# Optimizing a Trainium2 kernel written in Bass

```python
import numpy as np
import jax
import jax.numpy as jnp

def _softmax(x, axis=-1):
    return jax.nn.softmax(x, axis=axis)

def _gelu(x):
    return jax.nn.gelu(x, approximate=True)

def _silu(x):
    return jax.nn.silu(x)

def _sigmoid(x):
    return jax.nn.sigmoid(x)

def _layernorm(x, axis=-1, eps=1e-05):
    m = jnp.mean(x, axis=axis, keepdims=True)
    v = jnp.var(x, axis=axis, keepdims=True)
    return (x - m) / jnp.sqrt(v + eps)

def _scatter_add(tgt, idx, src, axis=0):
    return tgt.at[idx].add(src)

def _segment_sum(src, seg, n):
    return jax.ops.segment_sum(src, seg, n)
kernel_name = 'mk_prb_d1_jaxref_r4_55c6e7'

def setup_inputs(seed: int=0):
    np.random.seed(seed)
    _w = jnp.asarray

    def _L0_attn_setup():
        import jax, jax.numpy as jnp
        import numpy as np
        import math
        KSIZE = 4
        EPS_NORM = 1e-12
        EPS_LN = 1e-05

        def short_conv(x, w):
            b, l, c = x.shape
            K = w.shape[1]
            xp = jnp.pad(x, ((0, 0), (K - 1, 0), (0, 0)))
            y = x
            for j in range(K):
                y = y + xp[:, j:j + l, :] * w[:, j]
            return y

        def l2norm(x):
            return x * jax.lax.rsqrt(jnp.sum(x * x, axis=-1, keepdims=True) + EPS_NORM)

        def titans_forward(hidden_states, Wq, Wk, Wv, conv_q, conv_k, conv_v, W_init, ln_gamma, ln_beta, Wg, Wo, num_heads=16, chunk_size=16):
            b, l, dim = hidden_states.shape
            h = num_heads
            dk = dim // h
            cs = chunk_size
            nc = l // cs
            q = l2norm(jax.nn.silu(short_conv(hidden_states @ Wq.T, conv_q)).reshape(b, l, h, dk))
            k = l2norm(jax.nn.silu(short_conv(hidden_states @ Wk.T, conv_k)).reshape(b, l, h, dk))
            v = jax.nn.silu(short_conv(hidden_states @ Wv.T, conv_v)).reshape(b, l, h, dk)
            qc = q.reshape(b, nc, cs, h, dk).transpose(1, 0, 2, 3, 4)
            kc = k.reshape(b, nc, cs, h, dk).transpose(1, 0, 2, 3, 4)
            vc = v.reshape(b, nc, cs, h, dk).transpose(1, 0, 2, 3, 4)
            mask = jnp.tril(jnp.ones((cs, cs), q.dtype))
            W0 = jnp.broadcast_to(W_init, (b, h, dk, dk))

            def step(W, chunk):
                q_c, k_c, v_c = chunk
                inter = jnp.einsum('bqhk,bhkv->bqhv', q_c, W)
                qk = jnp.einsum('bqhd,bkhd->bhqk', q_c, k_c) * mask
                intra = jnp.einsum('bhqk,bkhv->bqhv', qk, v_c)
                W_new = W + jnp.einsum('bchk,bchv->bhkv', k_c, v_c)
                return (W_new, inter + intra)
            _, o = jax.lax.scan(step, W0, (qc, kc, vc))
            o = o.transpose(1, 0, 2, 3, 4).reshape(b, l, h, dk)
            mu = jnp.mean(o, axis=-1, keepdims=True)
            var = jnp.mean((o - mu) ** 2, axis=-1, keepdims=True)
            o = (o - mu) * jax.lax.rsqrt(var + EPS_LN) * ln_gamma + ln_beta
            o = o.reshape(b, l, dim)
            gate = hidden_states @ Wg.T
            return o * gate @ Wo.T
        key = jax.random.key(seed)
        ks = jax.random.split(key, 12)
        b, l, dim = (4, 512, 256)
        h = 16
        dk = dim // h
        s = 1.0 / math.sqrt(dim)
        inp = {'hidden_states': jax.random.normal(ks[0], (b, l, dim), jnp.float32), 'Wq': jax.random.normal(ks[1], (dim, dim), jnp.float32) * s, 'Wk': jax.random.normal(ks[2], (dim, dim), jnp.float32) * s, 'Wv': jax.random.normal(ks[3], (dim, dim), jnp.float32) * s, 'conv_q': jax.random.normal(ks[4], (dim, KSIZE), jnp.float32) * 0.1, 'conv_k': jax.random.normal(ks[5], (dim, KSIZE), jnp.float32) * 0.1, 'conv_v': jax.random.normal(ks[6], (dim, KSIZE), jnp.float32) * 0.1, 'W_init': jax.random.normal(ks[7], (1, h, dk, dk), jnp.float32) / math.sqrt(dk), 'ln_gamma': jnp.ones((dk,), jnp.float32), 'ln_beta': jnp.zeros((dk,), jnp.float32), 'Wg': jax.random.normal(ks[8], (dim, dim), jnp.float32) * s, 'Wo': jax.random.normal(ks[9], (dim, dim), jnp.float32) * s}
        return inp
    _L0_attn_in = _L0_attn_setup()

    def _L0_ffn_setup():
        import jax, jax.numpy as jnp
        import numpy as np
        IN_DIM = 256
        HIDDEN = 256
        OUT_DIM = 256
        NUM_EXPERTS = 16
        TOP_K = 2
        ROUTER_TEMP = 1.0
        LN_EPS = 1e-05

        def _layernorm(h, g, b):
            mu = jnp.mean(h, axis=-1, keepdims=True)
            var = jnp.mean(jnp.square(h - mu), axis=-1, keepdims=True)
            return (h - mu) * jax.lax.rsqrt(var + LN_EPS) * g + b
        key = jax.random.key(seed)
        ks = jax.random.split(key, 8)
        s_in = 1.0 / np.sqrt(IN_DIM)
        s_h = 1.0 / np.sqrt(HIDDEN)
        x = jax.random.normal(ks[0], (4, 512, IN_DIM), dtype=jnp.float32)
        Wr = jax.random.uniform(ks[1], (IN_DIM, NUM_EXPERTS), jnp.float32, -s_in, s_in)
        br = jax.random.uniform(ks[2], (NUM_EXPERTS,), jnp.float32, -s_in, s_in)
        W1 = jax.random.uniform(ks[3], (NUM_EXPERTS, IN_DIM, HIDDEN), jnp.float32, -s_in, s_in)
        b1 = jax.random.uniform(ks[4], (NUM_EXPERTS, HIDDEN), jnp.float32, -s_in, s_in)
        g1 = jnp.ones((NUM_EXPERTS, HIDDEN), jnp.float32)
        be1 = jnp.zeros((NUM_EXPERTS, HIDDEN), jnp.float32)
        W2 = jax.random.uniform(ks[5], (NUM_EXPERTS, HIDDEN, OUT_DIM), jnp.float32, -s_h, s_h)
        b2 = jax.random.uniform(ks[6], (NUM_EXPERTS, OUT_DIM), jnp.float32, -s_h, s_h)
        return {'x': x, 'Wr': Wr, 'br': br, 'W1': W1, 'b1': b1, 'g1': g1, 'be1': be1, 'W2': W2, 'b2': b2}
    _L0_ffn_in = _L0_ffn_setup()
    _d = {'L0_attn_hidden_states': _L0_attn_in['hidden_states'], 'L0_attn_Wq': _L0_attn_in['Wq'], 'L0_attn_Wk': _L0_attn_in['Wk'], 'L0_attn_Wv': _L0_attn_in['Wv'], 'L0_attn_conv_q': _L0_attn_in['conv_q'], 'L0_attn_conv_k': _L0_attn_in['conv_k'], 'L0_attn_conv_v': _L0_attn_in['conv_v'], 'L0_attn_W_init': _L0_attn_in['W_init'], 'L0_attn_ln_gamma': _L0_attn_in['ln_gamma'], 'L0_attn_ln_beta': _L0_attn_in['ln_beta'], 'L0_attn_Wg': _L0_attn_in['Wg'], 'L0_attn_Wo': _L0_attn_in['Wo'], 'L0_ffn_Wr': _L0_ffn_in['Wr'], 'L0_ffn_br': _L0_ffn_in['br'], 'L0_ffn_W1': _L0_ffn_in['W1'], 'L0_ffn_b1': _L0_ffn_in['b1'], 'L0_ffn_g1': _L0_ffn_in['g1'], 'L0_ffn_be1': _L0_ffn_in['be1'], 'L0_ffn_W2': _L0_ffn_in['W2'], 'L0_ffn_b2': _L0_ffn_in['b2']}
    _x0 = _d['L0_attn_hidden_states']
    _d['L0_attn_hidden_states'] = jax.random.normal(jax.random.fold_in(jax.random.key(seed), 1), (4, 2048, 256), dtype=_x0.dtype)
    del _x0
    return _d

def reference(L0_attn_hidden_states, L0_attn_Wq, L0_attn_Wk, L0_attn_Wv, L0_attn_conv_q, L0_attn_conv_k, L0_attn_conv_v, L0_attn_W_init, L0_attn_ln_gamma, L0_attn_ln_beta, L0_attn_Wg, L0_attn_Wo, L0_ffn_Wr, L0_ffn_br, L0_ffn_W1, L0_ffn_b1, L0_ffn_g1, L0_ffn_be1, L0_ffn_W2, L0_ffn_b2):

    def _L0_attn_ref(hidden_states, Wq, Wk, Wv, conv_q, conv_k, conv_v, W_init, ln_gamma, ln_beta, Wg, Wo):
        import jax, jax.numpy as jnp
        import numpy as np
        import math
        KSIZE = 4
        EPS_NORM = 1e-12
        EPS_LN = 1e-05

        def short_conv(x, w):
            b, l, c = x.shape
            K = w.shape[1]
            xp = jnp.pad(x, ((0, 0), (K - 1, 0), (0, 0)))
            y = x
            for j in range(K):
                y = y + xp[:, j:j + l, :] * w[:, j]
            return y

        def l2norm(x):
            return x * jax.lax.rsqrt(jnp.sum(x * x, axis=-1, keepdims=True) + EPS_NORM)

        def titans_forward(hidden_states, Wq, Wk, Wv, conv_q, conv_k, conv_v, W_init, ln_gamma, ln_beta, Wg, Wo, num_heads=16, chunk_size=16):
            b, l, dim = hidden_states.shape
            h = num_heads
            dk = dim // h
            cs = chunk_size
            nc = l // cs
            q = l2norm(jax.nn.silu(short_conv(hidden_states @ Wq.T, conv_q)).reshape(b, l, h, dk))
            k = l2norm(jax.nn.silu(short_conv(hidden_states @ Wk.T, conv_k)).reshape(b, l, h, dk))
            v = jax.nn.silu(short_conv(hidden_states @ Wv.T, conv_v)).reshape(b, l, h, dk)
            qc = q.reshape(b, nc, cs, h, dk).transpose(1, 0, 2, 3, 4)
            kc = k.reshape(b, nc, cs, h, dk).transpose(1, 0, 2, 3, 4)
            vc = v.reshape(b, nc, cs, h, dk).transpose(1, 0, 2, 3, 4)
            mask = jnp.tril(jnp.ones((cs, cs), q.dtype))
            W0 = jnp.broadcast_to(W_init, (b, h, dk, dk))

            def step(W, chunk):
                q_c, k_c, v_c = chunk
                inter = jnp.einsum('bqhk,bhkv->bqhv', q_c, W)
                qk = jnp.einsum('bqhd,bkhd->bhqk', q_c, k_c) * mask
                intra = jnp.einsum('bhqk,bkhv->bqhv', qk, v_c)
                W_new = W + jnp.einsum('bchk,bchv->bhkv', k_c, v_c)
                return (W_new, inter + intra)
            _, o = jax.lax.scan(step, W0, (qc, kc, vc))
            o = o.transpose(1, 0, 2, 3, 4).reshape(b, l, h, dk)
            mu = jnp.mean(o, axis=-1, keepdims=True)
            var = jnp.mean((o - mu) ** 2, axis=-1, keepdims=True)
            o = (o - mu) * jax.lax.rsqrt(var + EPS_LN) * ln_gamma + ln_beta
            o = o.reshape(b, l, dim)
            gate = hidden_states @ Wg.T
            return o * gate @ Wo.T
        return titans_forward(hidden_states, Wq, Wk, Wv, conv_q, conv_k, conv_v, W_init, ln_gamma, ln_beta, Wg, Wo)

    def _L0_ffn_ref(x, Wr, br, W1, b1, g1, be1, W2, b2):
        import jax, jax.numpy as jnp
        import numpy as np
        IN_DIM = 256
        HIDDEN = 256
        OUT_DIM = 256
        NUM_EXPERTS = 16
        TOP_K = 2
        ROUTER_TEMP = 1.0
        LN_EPS = 1e-05

        def _layernorm(h, g, b):
            mu = jnp.mean(h, axis=-1, keepdims=True)
            var = jnp.mean(jnp.square(h - mu), axis=-1, keepdims=True)
            return (h - mu) * jax.lax.rsqrt(var + LN_EPS) * g + b
        orig_shape = x.shape[:-1]
        x_flat = x.reshape(-1, x.shape[-1])
        logits = (x_flat @ Wr + br) / max(ROUTER_TEMP, 1e-06)
        probs = jax.nn.softmax(logits, axis=-1)
        topk_w, topk_idx = jax.lax.top_k(probs, TOP_K)
        topk_w = topk_w / jnp.clip(jnp.sum(topk_w, axis=-1, keepdims=True), 1e-09)
        h = jnp.einsum('nc,ech->neh', x_flat, W1) + b1
        h = _layernorm(h, g1, be1)
        h = jax.nn.gelu(h, approximate=False)
        expert_out = jnp.einsum('neh,eho->neo', h, W2) + b2
        sel = jnp.take_along_axis(expert_out, topk_idx[:, :, None], axis=1)
        y_flat = jnp.sum(sel * topk_w[:, :, None], axis=1)
        return y_flat.reshape(*orig_shape, y_flat.shape[-1])
    x = L0_attn_hidden_states
    xn = _layernorm(x, axis=-1)
    x = x + _L0_attn_ref(xn, L0_attn_Wq, L0_attn_Wk, L0_attn_Wv, L0_attn_conv_q, L0_attn_conv_k, L0_attn_conv_v, L0_attn_W_init, L0_attn_ln_gamma, L0_attn_ln_beta, L0_attn_Wg, L0_attn_Wo) + _L0_ffn_ref(xn, L0_ffn_Wr, L0_ffn_br, L0_ffn_W1, L0_ffn_b1, L0_ffn_g1, L0_ffn_be1, L0_ffn_W2, L0_ffn_b2)
    return x

_drawn_inputs = setup_inputs


def setup_inputs(seed=0):
    import zlib

    import numpy as np

    out = dict(_drawn_inputs(seed))
    spreads = {'L0_attn_ln_gamma': (1.0, 0.2),
     'L0_attn_ln_beta': (0.0, 0.1),
     'L0_ffn_g1': (1.0, 0.2),
     'L0_ffn_be1': (0.0, 0.432)}
    factors = {'L0_ffn_b1': 4.707, 'L0_ffn_b2': 3.294}
    for name, (base, spread) in spreads.items():
        noise = np.random.default_rng([zlib.crc32(name.encode()), seed]).standard_normal(out[name].shape)
        drawn = base * np.exp(spread * noise) if base else spread * noise
        out[name] = jnp.asarray(drawn.astype(out[name].dtype))
    for name, factor in factors.items():
        out[name] = (out[name] * factor).astype(out[name].dtype)
    return out
```

```python
from contextlib import ExitStack

import concourse.bass as bass
from concourse import mybir

F32 = mybir.dt.float32
F16 = mybir.dt.float16
I32 = mybir.dt.int32
ALU = mybir.AluOpType
ACT = mybir.ActivationFunctionType
X = mybir.AxisListType.X

P = 128
B, L, D = 4, 2048, 256
H, DK = 16, 16
NCH = L // P
W = B * P
NT = B * NCH
E, HID = 16, 256
SCALE_W = 64.0
UNSCALE = 1.0 / SCALE_W
EPS = 1e-5
EPS_NORM = 1e-12
SLOT_TILES = 144
GRP = 4
MAGIC = 1597463007.0

LINKS_A = 44
LINKS_B = 15
LINKS_F = 16


class Signal:

    def __init__(self, sem, per):
        self.sem, self.per = sem, per

    def at(self, i, k):
        return i * self.per + k

    def wait(self, eng, i, k):
        eng.wait_ge(self.sem, i * self.per + k)

    def wait_before(self, eng, i, back, k):
        if isinstance(i, int):
            if i - back < 0:
                return
        eng.wait_ge(self.sem, (i - back) * self.per + k if isinstance(i, int) else i * self.per + (k - back * self.per))


def apart(eng, passed):
    eng.sem_inc(passed, 1)


def after(u, par, by):
    return (u // 2 + 1) * by if isinstance(u, int) else u * (by // 2) + (by - par * (by // 2))


class Chain:

    def __init__(self, eng, sem, step, passed=None):
        self.eng, self.sem, self.step, self.i, self.n, self.passed = eng, sem, step, 0, 0, passed

    def start(self, i):
        self.i, self.n = i, 0

    def link(self, ins, next_apart=False):
        ins.then_inc(self.sem, 1)
        self.n += 1
        self.eng.wait_ge(self.sem, self.i * self.step + self.n)
        if next_apart:
            apart(self.eng, self.passed)

    def end(self):
        assert self.n == self.step, f"{self.sem}: {self.n} links, not {self.step}"


def inverse_sqrt(nc, chain, y, x, t, guess):
    chain.link(nc.vector.tensor_scalar(guess, x.bitcast(I32), 1, None, ALU.arith_shift_right))
    chain.link(nc.vector.tensor_scalar(guess, guess, -1.0, MAGIC, ALU.mult, ALU.add))
    src = guess.bitcast(F32)
    for _ in range(3):
        chain.link(nc.vector.tensor_tensor(t, src, src, ALU.mult))
        chain.link(nc.vector.scalar_tensor_tensor(out=t, in0=t, scalar=-0.5, in1=x, op0=ALU.mult, op1=ALU.mult))
        chain.link(nc.vector.scalar_tensor_tensor(out=y, in0=t, scalar=1.5, in1=src, op0=ALU.add, op1=ALU.mult))
        src = y


def program(nc, a, debug=False):
    x_d, out_d = a["x"], a["out"]
    xn_d, attn_d = a["xn_rows"], a["attn_rows"]
    ctx = ExitStack()
    with ctx:
        def sb(name, shape, dt=F32, c=ctx):
            return c.enter_context(nc.sbuf_tensor(name, shape, dt))

        def sem(name, c=ctx):
            return c.enter_context(nc.semaphore(name))

        ident = sb("ident", [P, P])
        logits = sb("logits", [P, NT, E])

        wts = sb("wts", [P, 2, NT])
        slots = sb("slots", [P, 2, NT], I32)
        attention(nc, a, sb, sem, ident, logits)
        mid = ExitStack()
        with mid:
            ids = sb("ids", [P, SLOT_TILES], I32, mid)
            eid = sb("eid", [P, SLOT_TILES], I32, mid)
            w1h, w1l = sb("w1h", [P, E, 2, HID], F16, mid), sb("w1l", [P, E, 2, HID], F16, mid)
            w2h, w2l = sb("w2h", [P, E, 2, D], F16, mid), sb("w2l", [P, E, 2, D], F16, mid)
            brow = sb("brow", [3, 2, E, D], F16, mid)
            ones3 = sb("ones3", [3, P], F16, mid)
            kept = (ids, eid, w1h, w1l, w2h, w2l, brow, ones3)
            routing(nc, a, sb, sem, ident, logits, wts, slots, *kept)
            experts(nc, a, sb, sem, ident, *kept)
        combine(nc, a, sb, sem, wts, slots)


def attention(nc, a, sb_, sem_, ident, logits):
    ctx = ExitStack()
    with ctx:
        def sb(name, shape, dt=F32):
            return sb_(name, shape, dt, ctx)

        def sem(name):
            return sem_(name, ctx)

        wh = sb("wh", [P, 5, 2, D], F16)
        wl = sb("wl", [P, 5, 2, D], F16)
        rh = sb("rh", [P, 2, E], F16)
        rl = sb("rl", [P, 2, E], F16)
        taps = sb("taps", [P, 6, 4])
        gam = sb("gam", [P, 1])
        bet = sb("bet", [P, 1])
        br = sb("br", [P, E])
        cmask = sb("cmask", [P, 192])
        bdmask = sb("bdmask", [P, P])
        parity = sb("parity", [P, 2])
        state = sb("state", [P, B, 2, P])

        xs = sb("xs", [P, B, D])
        stats = sb("stats", [P, B, 6])
        mv = sb("mv", [P, B, 2])
        rstd = sb("rstd", [P, B])
        nbias = sb("nbias", [P, B])
        xn = sb("xn", [P, B, D])
        xh = sb("xh", [P, 2, W], F16)
        xl = sb("xl", [P, 2, W], F16)
        pre = sb("pre", [P, 6, B, P + 3])
        acc = sb("acc", [P, 2, W])
        kt = sb("kt", [P, 2, W])
        vt = sb("vt", [P, 2, W])
        khf = sb("khf", [P, 2, W], F16)
        klf = sb("klf", [P, 2, W], F16)
        sq = sb("sq", [P, 2, W])
        ssq = sb("ssq", [P, B, 32])
        rk = sb("rk", [P, B * H])
        ta = sb("ta", [P, B * H])
        ga = sb("ga", [P, B * H], I32)
        qt = [sb(f"qt{n}", [P, 2, W]) for n in range(2)]
        qh = [sb(f"qh{n}", [P, 2, W], F16) for n in range(2)]
        ql = [sb(f"ql{n}", [P, 2, W], F16) for n in range(2)]
        kmh = [sb(f"kmh{n}", [P, 2, 8, 2, 64], F16) for n in range(2)]
        kml = [sb(f"kml{n}", [P, 2, 8, 2, 64], F16) for n in range(2)]
        gate = [sb(f"gate{n}", [P, 2, W]) for n in range(2)]
        kn = [sb(f"kn{n}", [P, B, D]) for n in range(2)]
        vp = [sb(f"vp{n}", [P, B, D]) for n in range(2)]
        vbd = [sb(f"vbd{n}", [P, B, 2, 8, 32]) for n in range(2)]
        epsq = [sb(f"epsq{n}", [P, B * H]) for n in range(2)]
        sc = [sb(f"sc{n}", [P, 4, 192]) for n in range(2)]
        um = [sb(f"um{n}", [P, 2, P]) for n in range(2)]
        ot = sb("ot", [P, 2, W])
        osum = sb("osum", [P, B * H])
        oc = sb("oc", [P, B * D])
        osq = sb("osq", [P, B * D])
        ro = sb("ro", [P, B * H])
        tb = sb("tb", [P, B * H])
        gb = sb("gb", [P, B * H], I32)
        og = sb("og", [P, 2, W])
        ogh = sb("ogh", [P, 2, W], F16)
        ogl = sb("ogl", [P, 2, W], F16)
        at = sb("at", [P, B, D])

        bank = [ctx.enter_context(nc.psum_tensor(f"bank{n}", [P, W], F32)) for n in range(2)]
        sbank = ctx.enter_context(nc.psum_tensor("sbank", [P, 4, W], F32))
        oubank = [ctx.enter_context(nc.psum_tensor(f"oubank{n}", [P, W], F32)) for n in range(2)]

        loaded, loaded_r, split_h, split_l, ready = (sem(s) for s in ("loaded", "loaded_r", "split_h", "split_l", "ready"))
        loaded_w = [sem(f"loaded_w{n}") for n in range(2)]
        wf = [osq, oc]
        wide = [a["wat"][m] for m in range(5)]

        with nc.Block() as block:
            @block.sync
            def _(sp):
                for dst, src in ((ident, "ident"), (taps, "taps"), (gam, "gam"), (bet, "bet"), (br, "br"),
                                 (cmask, "cmask"), (bdmask, "bdmask"), (parity, "parity"), (state, "winit")):
                    sp.dma_start(dst[:], a[src]).then_inc(loaded, 16)
                for m in range(5):
                    if m >= 2:
                        sp.wait_ge(split_l, m - 1)
                    sp.dma_start(wf[m % 2][:, 0:512].rearrange("p (h n) -> p h n", h=2), wide[m]).then_inc(loaded_w[m % 2], 16)
                sp.dma_start(sq[:, 0, 0:2 * E].rearrange("p (h n) -> p h n", h=2), a["wr"]).then_inc(loaded_r, 16)
                sp.wait_ge(loaded, 9 * 16)

            @block.scalar
            def _(act):
                for m in range(5):
                    act.wait_ge(loaded_w[m % 2], 16 * (m // 2 + 1))
                    act.activation(wh[:, m, :, :].rearrange("p h n -> p (h n)"), wf[m % 2][:, 0:512], ACT.Copy,
                                   scale=SCALE_W).then_inc(split_h, 1)
                act.wait_ge(loaded_r, 16)
                act.activation(rh[:].rearrange("p h n -> p (h n)"), sq[:, 0, 0:2 * E], ACT.Copy,
                               scale=SCALE_W).then_inc(split_h, 1)

            @block.vector
            def _(dve):
                for m in range(5):
                    dve.wait_ge(split_h, m + 1)
                    dve.wait_ge(loaded_w[m % 2], 16 * (m // 2 + 1))
                    dve.scalar_tensor_tensor(out=wl[:, m, :, :].rearrange("p h n -> p (h n)"), in0=wf[m % 2][:, 0:512],
                                             scalar=SCALE_W, in1=wh[:, m, :, :].rearrange("p h n -> p (h n)"),
                                             op0=ALU.mult, op1=ALU.subtract).then_inc(split_l, 1)
                dve.wait_ge(split_h, 6)
                dve.wait_ge(loaded_r, 16)
                dve.scalar_tensor_tensor(out=rl[:].rearrange("p h n -> p (h n)"), in0=sq[:, 0, 0:2 * E], scalar=SCALE_W,
                                         in1=rh[:].rearrange("p h n -> p (h n)"),
                                         op0=ALU.mult, op1=ALU.subtract).then_inc(split_l, 1)
                dve.wait_ge(loaded, 9 * 16)
                dve.tensor_scalar(taps[:, :, 3], taps[:, :, 3], 1.0, None, ALU.add).then_inc(ready, 1)
                dve.memset(pre[:], 0.0).then_inc(ready, 1)

            @block.gpsimd
            def _(pool):
                for n in range(2):
                    pool.memset(vbd[n][:], 0.0).then_inc(ready, 1)
                pool.wait_ge(ready, 4)

        def sig(name, per):
            return Signal(sem(name), per)

        x_in, xn_out, at_out = sig("x_in", 16), sig("xn_out", 16), sig("at_out", 16)
        s_rstd, s_xn, s_xt, s_xh, s_xl = sig("rstd_ok", 1), sig("xn_ok", 4), sig("xt_ok", 2), sig("xh_ok", 2), sig("xl_ok", 2)
        s_lg, s_lge = sig("logit_mm", 1), sig("logit_ok", 1)
        s_proj, s_p, s_g = sig("proj_mm", 8), sig("pre_ok", 6), sig("gate_ok", 2)
        s_tap, s_conv, s_hist, s_silu = sig("tap_ok", 6), sig("conv_ok", 6), sig("hist_ok", 1), sig("silu_ok", 6)
        s_qkt, s_kn, s_sq, s_ssq = sig("qkt_ok", 4), sig("kn_ok", 4), sig("sq_ok", 4), sig("ssq_ok", 4)
        s_vtt, s_vp, s_vbd, s_epsq = sig("vt_ok", 2), sig("vp_ok", 2), sig("vbd_ok", 4), sig("epsq_ok", 1)
        s_qh, s_ql, s_kh, s_kl, s_km = sig("qh_ok", 2), sig("ql_ok", 2), sig("kh_ok", 2), sig("kl_ok", 2), sig("km_ok", 8)
        s_s, s_sc, s_o, s_oe = sig("score_mm", 8), sig("score_ok", 8), sig("o_mm", 8), sig("o_out", 4)
        s_u, s_um, s_st = sig("u_mm", 4), sig("um_ok", 4), sig("state_ok", 4)
        s_on, s_oc, s_osq, s_onn, s_ont = sig("on_t", 1), sig("oc_ok", 1), sig("osq_ok", 1), sig("onorm_ok", 1), sig("onorm_t", 1)
        s_oga, s_ogg, s_ogh, s_ogl = sig("oga_ok", 2), sig("ogg_ok", 2), sig("ogh_ok", 2), sig("ogl_ok", 2)
        s_wo, s_at = sig("wo_mm", 1), sig("at_ok", 2)
        chain_a, chain_b, passed = sem("chain_a"), sem("chain_b"), sem("passed_a")

        def steps(eng, front, both, back):
            front(0, 0)
            both(0, 0)
            both(1, 1)
            with eng.Fori(1, NCH // 2 - 1) as k:
                both(k * 2, 0)
                both(k * 2 + 1, 1)
            both(NCH - 2, 0)
            back(NCH - 1, 1)

        def run_pieces(eng, a_pieces, b_pieces):
            def front(i, par):
                for f in a_pieces(i, par):
                    f()

            def back(i, par):
                for f in b_pieces(i, par):
                    f()

            def both(i, par):
                fa, fb = a_pieces(i + 1, 1 - par), b_pieces(i, par)
                for k in range(max(len(fa), len(fb))):
                    if k < len(fb):
                        fb[k]()
                    if k < len(fa):
                        fa[k]()
            steps(eng, front, both, back)

        nothing = lambda: None
        block = ctx.enter_context(nc.Block())

        @block.sync
        def _(sp):
            def a_pieces(i, par):
                def load():
                    s_xn.wait_before(sp, i, 1, 4)
                    apart(sp, passed)
                    sp.dma_start(xs[:], a["x"][:, bass.ds(i * P, P), :].rearrange("b t c -> t b c")).then_inc(x_in.sem, 16)

                def store():
                    s_xn.wait(sp, i, 4)
                    apart(sp, passed)
                    sp.dma_start(a["xn_rows"][:, bass.ds(i * P, P), :].rearrange("b t c -> t b c"), xn[:]).then_inc(xn_out.sem, 16)
                return [load, store]

            def b_pieces(i, par):
                def store():
                    s_at.wait(sp, i, 2)
                    apart(sp, passed)
                    sp.dma_start(a["attn_rows"][:, bass.ds(i * P, P), :].rearrange("b t c -> t b c"), at[:]).then_inc(at_out.sem, 16)
                return [nothing, nothing, store]
            run_pieces(sp, a_pieces, b_pieces)
            xn_out.wait(sp, NCH - 1, 16)
            at_out.wait(sp, NCH - 1, 16)

        @block.vector
        def _(dve):
            ca, cb = Chain(dve, chain_a, LINKS_A, passed), Chain(dve, chain_b, LINKS_B)

            def a_pieces(i, par):
                def norm():
                    ca.start(i)
                    x_in.wait(dve, i, 16)
                    s_xn.wait_before(dve, i, 1, 4)
                    for b in range(B):
                        ca.link(nc.vector.bn_stats(stats[:, b, :], xs[:, b, :]), True)
                    for b in range(B):
                        ca.link(nc.vector.bn_aggr(mv[:, b, :], stats[:, b, :]), True)
                    ca.link(nc.vector.tensor_scalar(ta[:, 0:B], mv[:, :, 1], EPS, None, ALU.add))
                    inverse_sqrt(nc, ca, rstd[:], ta[:, 0:B], ta[:, B:2 * B], ga[:, 0:B])
                    nc.vector.scalar_tensor_tensor(out=nbias[:], in0=mv[:, :, 0], scalar=-1.0, in1=rstd[:],
                                                   op0=ALU.mult, op1=ALU.mult).then_inc(s_rstd.sem, 1)

                def low():
                    for h in range(2):
                        s_xh.wait(dve, i, h + 1)
                        nc.vector.tensor_tensor(xl[:, h, :], bank[h][:], xh[:, h, :], ALU.subtract).then_inc(s_xl.sem, 1)

                def logit():
                    s_lg.wait(dve, i, 1)
                    nc.vector.scalar_tensor_tensor(
                        out=logits[:, bass.ds(i * B, B), :], in0=bank[0][:, 0:B * E].rearrange("p (b e) -> p b e", b=B),
                        scalar=UNSCALE, in1=br[:, None, :].to_broadcast([P, B, E]),
                        op0=ALU.mult, op1=ALU.add).then_inc(s_lge.sem, 1)

                def conv(blks):
                    for blk in blks:
                        s_tap.wait(dve, i, blk + 1)
                        c = acc[:, blk % 2, :].rearrange("p (b t) -> p b t", b=B)
                        for j in range(3):
                            ins = nc.vector.scalar_tensor_tensor(out=c, in0=pre[:, blk, :, j:j + P], scalar=taps[:, blk, j:j + 1],
                                                                 in1=c, op0=ALU.mult, op1=ALU.add)
                            if j < 2:
                                ca.link(ins)
                            else:
                                ins.then_inc(s_conv.sem, 1)
                    if blks[-1] == 5:
                        s_conv.wait(dve, i, 6)
                        nc.vector.tensor_copy(pre[:, :, :, 0:3].rearrange("p k b t -> p (k b) t"),
                                              pre[:, :, :, P:P + 3].rearrange("p k b t -> p (k b) t")).then_inc(s_hist.sem, 1)

                def masks():
                    for n, (src, dst, ok) in enumerate(((khf, kmh, s_kh), (klf, kml, s_kl))):
                        for o in range(2):
                            ok.wait(dve, i, o + 1)
                            if n == 0 and o == 0:
                                s_s.wait_before(dve, i, 2, 8)
                            for e in range(2):
                                nc.vector.tensor_scalar(dst[par][:, o, :, e, :], src[:, o, :].rearrange("p (k s) -> p k s", s=64),
                                                        parity[:, e:e + 1], None, ALU.mult).then_inc(s_km.sem, 1)

                def norms():
                    for b in range(B):
                        s_sq.wait(dve, i, b + 1)
                        nc.vector.reduce_sum(ssq[:, b, :], sq[:, b % 2, :].rearrange("p (h k) -> p h k", k=DK),
                                             axis=X).then_inc(s_ssq.sem, 1)
                    s_ssq.wait(dve, i, B)
                    s_onn.wait_before(dve, i, 2, 1)
                    nc.vector.tensor_scalar(epsq[par][:].rearrange("p (b h) -> p b h", b=B), ssq[:, :, 0:H], EPS_NORM, EPS,
                                            ALU.add, ALU.mult).then_inc(s_epsq.sem, 1)
                    ca.link(nc.vector.tensor_scalar(ta[:].rearrange("p (b h) -> p b h", b=B), ssq[:, :, H:2 * H], EPS_NORM, None, ALU.add))
                    inverse_sqrt_t(ca)

                def inverse_sqrt_t(c):
                    inverse_sqrt(nc, c, rk[:], ta[:], sq[:, 0, 0:B * H], ga[:])

                def values():
                    for n in range(2):
                        s_vtt.wait(dve, i, n + 1)
                        if n == 0:
                            s_u.wait_before(dve, i, 2, 4)
                            s_vbd.wait_before(dve, i, 2, 4)
                        nc.vector.tensor_tensor(vp[par][:, 2 * n:2 * n + 2, :].rearrange("p b (h k) -> p (b h) k", k=DK),
                                                bank[1 - n][:].rearrange("p (h k) -> p h k", k=DK),
                                                rk[:, 2 * n * H:(2 * n + 2) * H][:, :, None].to_broadcast([P, 2 * H, DK]),
                                                ALU.mult).then_inc(s_vp.sem, 1)
                    ca.end()
                return [norm, low, logit, lambda: conv([0, 1]), lambda: conv([2, 3]), lambda: conv([4, 5]), nothing,
                        nothing, nothing, masks, lambda: (norms(), values())]

            def b_pieces(i, par):
                def unit(t):
                    b, h = divmod(t, 2)
                    if t == 0:
                        cb.start(i)
                    s_s.wait(dve, i, t + 1)
                    if t < 2:
                        s_o.wait_before(dve, i, 1, 7 + t)
                    else:
                        s_o.wait(dve, i, t - 1)
                    nc.vector.tensor_tensor(sc[t % 2][:], sbank[:, :, 0:192], cmask[:, None, :].to_broadcast([P, 4, 192]),
                                            ALU.mult).then_inc(s_sc.sem, 1)
                    if h == 0 and b > 0:
                        update(b - 1)

                def update(b):
                    s_u.wait(dve, i, b + 1)
                    s_oe.wait(dve, i, b + 1)
                    if b < 2:
                        s_st.wait_before(dve, i, 1, 3 + b)
                    else:
                        s_st.wait(dve, i, b - 1)
                    nc.vector.tensor_tensor(um[b % 2][:], oubank[b % 2][:, 256:512].rearrange("p (h n) -> p h n", h=2),
                                            bdmask[:, None, :].to_broadcast([P, 2, P]), ALU.mult).then_inc(s_um.sem, 1)

                def centre():
                    update(B - 1)
                    s_on.wait(dve, i, 1)
                    full = sbank[:, 0:2, :].rearrange("p k (h v) -> p (k h) v", v=DK)
                    cb.link(nc.vector.reduce_sum(osum[:], full, axis=X))
                    cb.link(nc.vector.tensor_scalar(osum[:], osum[:], 1.0 / DK, None, ALU.mult))
                    nc.vector.tensor_tensor(oc[:].rearrange("p (h v) -> p h v", v=DK), full,
                                            osum[:][:, :, None].to_broadcast([P, B * H, DK]), ALU.subtract).then_inc(s_oc.sem, 1)

                def scale():
                    s_osq.wait(dve, i, 1)
                    cb.link(nc.vector.reduce_sum(ro[:], osq[:].rearrange("p (h v) -> p h v", v=DK), axis=X))
                    s_epsq.wait(dve, i, 1)
                    cb.link(nc.vector.scalar_tensor_tensor(out=osum[:], in0=ro[:], scalar=1.0 / DK, in1=epsq[par][:],
                                                           op0=ALU.mult, op1=ALU.add))
                    inverse_sqrt(nc, cb, ro[:], osum[:], tb[:], gb[:])
                    nc.vector.tensor_tensor(oc[:].rearrange("p (h v) -> p h v", v=DK), oc[:].rearrange("p (h v) -> p h v", v=DK),
                                            ro[:][:, :, None].to_broadcast([P, B * H, DK]), ALU.mult).then_inc(s_onn.sem, 1)

                def gated():
                    for h in range(2):
                        s_oga.wait(dve, i, h + 1)
                        nc.vector.tensor_tensor(og[:, h, :], og[:, h, :], gate[par][:, h, :], ALU.mult).then_inc(s_ogg.sem, 1)
                    cb.end()
                return [lambda t=t: unit(t) for t in range(8)] + [centre, scale, gated]
            run_pieces(dve, a_pieces, b_pieces)

        @block.scalar
        def _(act):
            def a_pieces(i, par):
                def norm():
                    s_rstd.wait(act, i, 1)
                    xn_out.wait_before(act, i, 1, 16)
                    s_xt.wait_before(act, i, 1, 2)
                    for b in range(B):
                        act.activation(xn[:, b, :], xs[:, b, :], ACT.Identity, scale=rstd[:, b:b + 1],
                                       bias=nbias[:, b:b + 1]).then_inc(s_xn.sem, 1)

                def high():
                    for h in range(2):
                        s_xt.wait(act, i, h + 1)
                        if h == 0:
                            s_proj.wait_before(act, i, 1, 8)
                        act.activation(xh[:, h, :], bank[h][:], ACT.Copy).then_inc(s_xh.sem, 1)

                def evac(blks):
                    for blk in blks:
                        s_proj.wait(act, i, blk + 1)
                        if blk == 0:
                            s_hist.wait_before(act, i, 1, 1)
                        act.activation(pre[:, blk, :, 3:], bank[(blk + 1) % 2][:].rearrange("p (b t) -> p b t", b=B), ACT.Copy,
                                       scale=UNSCALE).then_inc(s_p.sem, 1)

                def evac_gate():
                    for h in range(2):
                        s_proj.wait(act, i, 7 + h)
                        if h == 0:
                            s_ogg.wait_before(act, i, 2, 2)
                        act.activation(gate[par][:, h, :], bank[(h + 1) % 2][:], ACT.Copy, scale=UNSCALE).then_inc(s_g.sem, 1)

                def silu(blks):
                    for blk in blks:
                        s_conv.wait(act, i, blk + 1)
                        dst = (qt[par], kt, vt)[blk // 2]
                        if blk == 0:
                            s_o.wait_before(act, i, 2, 8)
                            s_ql.wait_before(act, i, 2, 2)
                        if blk == 2:
                            s_qkt.wait_before(act, i, 1, 4)
                            s_kl.wait_before(act, i, 1, 2)
                        if blk == 4:
                            s_vtt.wait_before(act, i, 1, 2)
                        act.activation(dst[:, blk % 2, :], acc[:, blk % 2, :], ACT.Silu).then_inc(s_silu.sem, 1)

                def halves():
                    for h in range(2):
                        s_silu.wait(act, i, h + 1)
                        if h == 0:
                            s_s.wait_before(act, i, 2, 8)
                        act.activation(qh[par][:, h, :], qt[par][:, h, :], ACT.Copy).then_inc(s_qh.sem, 1)
                    for h in range(2):
                        s_silu.wait(act, i, h + 3)
                        if h == 0:
                            s_km.wait_before(act, i, 1, 8)
                        act.activation(khf[:, h, :], kt[:, h, :], ACT.Copy).then_inc(s_kh.sem, 1)

                def squares():
                    for b in range(B):
                        s_qkt.wait(act, i, b + 1)
                        if b == 0:
                            s_u.wait_before(act, i, 2, 4)
                        if b < 2:
                            s_ssq.wait_before(act, i, 1, 3 + b)
                            s_vp.wait_before(act, i, 1, 2)
                        else:
                            s_ssq.wait(act, i, b - 1)
                        act.activation(kn[par][:, b, :], bank[(b + 1) % 2][:, 256:512], ACT.Copy).then_inc(s_kn.sem, 1)
                        act.activation(sq[:, b % 2, :], bank[(b + 1) % 2][:], ACT.Square).then_inc(s_sq.sem, 1)

                def spread():
                    s_vp.wait(act, i, 2)
                    s_o.wait_before(act, i, 2, 8)
                    for s in range(2):
                        for e in range(2):
                            src = vp[par][64 * s:64 * s + 64, :, :].rearrange("p b (k e v) -> p (b k) e v", e=2, v=DK)[:, :, e, :]
                            dst = vbd[par][64 * e:64 * e + 64, :, s, :, 16 * e:16 * e + 16]
                            act.activation(dst, src.rearrange("p (b k) v -> p b k v", b=B), ACT.Copy).then_inc(s_vbd.sem, 1)
                return [norm, high, nothing, lambda: (evac([0, 1]), silu([0])), lambda: (evac([2, 3]), silu([1, 2])),
                        lambda: (evac([4, 5]), silu([3, 4])), lambda: (evac_gate(), silu([5]), halves()),
                        nothing, nothing, squares, spread]

            def b_pieces(i, par):
                def out(b):
                    s_u.wait(act, i, b + 1)
                    if b == 0:
                        s_on.wait_before(act, i, 1, 1)
                    act.activation(ot[:, :, b * P:(b + 1) * P], oubank[b % 2][:, 0:256].rearrange("p (h t) -> p h t", h=2),
                                   ACT.Copy).then_inc(s_oe.sem, 1)

                def square():
                    s_oc.wait(act, i, 1)
                    act.activation(osq[:], oc[:], ACT.Square).then_inc(s_osq.sem, 1)

                def affine():
                    s_ont.wait(act, i, 1)
                    s_ogl.wait_before(act, i, 1, 2)
                    for h in range(2):
                        act.activation(og[:, h, :], sbank[:, 2 + h, :], ACT.Identity, scale=gam[:], bias=bet[:]).then_inc(s_oga.sem, 1)
                    for h in range(2):
                        s_ogg.wait(act, i, h + 1)
                        if h == 0:
                            s_wo.wait_before(act, i, 1, 1)
                        act.activation(ogh[:, h, :], og[:, h, :], ACT.Copy).then_inc(s_ogh.sem, 1)

                def evac():
                    s_wo.wait(act, i, 1)
                    at_out.wait_before(act, i, 1, 16)
                    for n in range(2):
                        act.activation(at[:, 2 * n:2 * n + 2, :], sbank[:, n, :].rearrange("p (b c) -> p b c", b=2), ACT.Copy,
                                       scale=UNSCALE).then_inc(s_at.sem, 1)
                return [nothing, nothing, lambda: out(0), nothing, lambda: out(1), nothing, lambda: out(2), nothing,
                        lambda: (out(3), square()), affine, evac]
            run_pieces(act, a_pieces, b_pieces)

        @block.gpsimd
        def _(pool):
            def a_pieces(i, par):
                def tap(blks):
                    for blk in blks:
                        s_p.wait(pool, i, blk + 1)
                        if blk < 2:
                            s_silu.wait_before(pool, i, 1, 5 + blk)
                        else:
                            s_silu.wait(pool, i, blk - 1)
                        apart(pool, passed)
                        pool.tensor_scalar(acc[:, blk % 2, :].rearrange("p (b t) -> p b t", b=B), pre[:, blk, :, 3:],
                                           taps[:, blk, 3:4], None, ALU.mult).then_inc(s_tap.sem, 1)

                def lows():
                    for h in range(2):
                        s_qh.wait(pool, i, h + 1)
                        if h == 0:
                            s_s.wait_before(pool, i, 2, 8)
                        pool.tensor_tensor(ql[par][:, h, :], qt[par][:, h, :], qh[par][:, h, :], ALU.subtract).then_inc(s_ql.sem, 1)
                    for h in range(2):
                        s_kh.wait(pool, i, h + 1)
                        if h == 0:
                            s_km.wait_before(pool, i, 1, 8)
                        pool.tensor_tensor(klf[:, h, :], kt[:, h, :], khf[:, h, :], ALU.subtract).then_inc(s_kl.sem, 1)
                return [nothing, nothing, nothing, lambda: tap([0, 1]), lambda: tap([2, 3]), lambda: tap([4, 5]), lows]

            def b_pieces(i, par):
                def add(b):
                    s_um.wait(pool, i, b + 1)
                    s_st.wait_before(pool, i, 1, b + 1)
                    pool.tensor_tensor(state[:, b, :, :], state[:, b, :, :], um[b % 2][:], ALU.add).then_inc(s_st.sem, 1)

                def low():
                    for h in range(2):
                        s_ogh.wait(pool, i, h + 1)
                        if h == 0:
                            s_wo.wait_before(pool, i, 1, 1)
                        pool.tensor_tensor(ogl[:, h, :], og[:, h, :], ogh[:, h, :], ALU.subtract).then_inc(s_ogl.sem, 1)
                return [nothing, nothing, nothing, lambda: add(0), nothing, lambda: add(1), nothing, lambda: add(2), lambda: add(3), low]
            run_pieces(pool, a_pieces, b_pieces)

        @block.tensor
        def _(pe):
            mm = nc.tensor.matmul

            def a_pieces(i, par):
                def flip():
                    s_xn.wait(pe, i, 4)
                    for h in range(2):
                        s_vp.wait_before(pe, i, 1, 2 - h)
                        for b in range(B):
                            last = nc.tensor.transpose(bank[h][:, b * P:(b + 1) * P], xn[:, b, h * P:(h + 1) * P], ident[:])
                        last.then_inc(s_xt.sem, 1)

                def route():
                    s_xl.wait(pe, i, 2)
                    for b in range(B):
                        n = 0
                        for lhs, rhs in ((xh, rh), (xh, rl), (xl, rh)):
                            for h in range(2):
                                last = mm(bank[0][:, b * E:(b + 1) * E], lhs[:, h, b * P:(b + 1) * P], rhs[:, h, :],
                                          start=n == 0, stop=n == 5)
                                n += 1
                    last.then_inc(s_lg.sem, 1)

                def project(blks):
                    for blk in blks:
                        m, o = divmod(blk, 2)
                        if blk == 0:
                            s_xl.wait(pe, i, 2)
                        elif blk == 1:
                            s_lge.wait(pe, i, 1)
                        else:
                            (s_p if blk - 2 < 6 else s_g).wait(pe, i, blk - 1)
                        n = 0
                        for lhs, rhs in ((wh, xh), (wl, xh), (wh, xl)):
                            for h in range(2):
                                last = mm(bank[(blk + 1) % 2][:], lhs[:, m, h, o * P:(o + 1) * P], rhs[:, h, :],
                                          start=n == 0, stop=n == 5)
                                n += 1
                        last.then_inc(s_proj.sem, 1)

                def to_rows():
                    s_silu.wait(pe, i, 4)
                    for b in range(B):
                        if b < 2:
                            s_g.wait(pe, i, b + 1)
                        else:
                            s_sq.wait(pe, i, b - 1)
                            s_kn.wait(pe, i, b - 1)
                        for n, src in enumerate((qt[par], kt)):
                            for h in range(2):
                                last = nc.tensor.transpose(bank[(b + 1) % 2][:, n * 256 + h * P:n * 256 + (h + 1) * P],
                                                           src[:, h, b * P:(b + 1) * P], ident[:])
                        last.then_inc(s_qkt.sem, 1)
                    s_silu.wait(pe, i, 6)
                    for n in range(2):
                        s_sq.wait(pe, i, n + 3)
                        for b in range(2):
                            for h in range(2):
                                last = nc.tensor.transpose(bank[1 - n][:, b * 256 + h * P:b * 256 + (h + 1) * P],
                                                           vt[:, h, (2 * n + b) * P:(2 * n + b + 1) * P], ident[:])
                        last.then_inc(s_vtt.sem, 1)
                return [flip, route, lambda: project([0, 1]), lambda: project([2, 3]), lambda: project([4, 5]),
                        lambda: project([6, 7]), nothing, nothing, nothing, to_rows]

            def b_pieces(i, par):
                def scores(t):
                    b, h = divmod(t, 2)
                    if t == 0:
                        s_km.wait(pe, i, 8)
                        s_ql.wait(pe, i, 2)
                        s_qh.wait(pe, i, 2)
                        s_at.wait_before(pe, i, 1, 2)
                    else:
                        s_sc.wait(pe, i, t)
                    for r in range(4):
                        rows = slice(32 * r, 32 * r + 32)
                        n = 0
                        for km, q in ((kmh, qh), (kmh, ql), (kml, qh)):
                            mm(sbank[:, r, 0:P], km[par][rows, h, 2 * b, :, :].rearrange("p e s -> p (e s)"),
                               q[par][rows, h, b * P:(b + 1) * P], start=n == 0, stop=n == 2)
                            n += 1
                        n = 0
                        for km, q in ((kmh, qh), (kmh, ql), (kml, qh)):
                            last = mm(sbank[:, r, P:192], km[par][rows, h, 2 * b + 1, :, :].rearrange("p e s -> p (e s)"),
                                      q[par][rows, h, b * P + 64:(b + 1) * P], start=n == 0, stop=n == 2)
                            n += 1
                    last.then_inc(s_s.sem, 1)

                def outputs(t):
                    b, h = divmod(t, 2)
                    if h == 0:
                        s_st.wait_before(pe, i, 1, b + 1)
                        if b < 2:
                            s_um.wait_before(pe, i, 1, 3 + b)
                        else:
                            s_um.wait(pe, i, b - 1)
                    if t == 0:
                        s_vbd.wait(pe, i, 4)
                        s_kn.wait(pe, i, 4)
                    s_sc.wait(pe, i, t + 1)
                    o = oubank[b % 2]
                    mm(o[:, h * P:(h + 1) * P], state[:, b, h, :], qt[par][:, h, b * P:(b + 1) * P],
                       start=True, stop=False, skip_group_check=True)
                    for r in range(4):
                        rows = slice(32 * r, 32 * r + 32)
                        mm(o[rows, h * P:(h + 1) * P], vbd[par][:, b, 0, 4 * h + r, :], sc[t % 2][:, r, 0:P],
                           start=False, stop=False, skip_group_check=True)
                        last = mm(o[rows, h * P + 64:(h + 1) * P], vbd[par][:, b, 1, 4 * h + r, :], sc[t % 2][:, r, P:192],
                                  start=False, stop=True, skip_group_check=True)
                    last.then_inc(s_o.sem, 1)
                    if h == 1:
                        for g in range(2):
                            last = mm(o[:, 256 + g * P:256 + (g + 1) * P], kn[par][:, b, g * P:(g + 1) * P],
                                      vp[par][:, b, g * P:(g + 1) * P], start=True, stop=True)
                        last.then_inc(s_u.sem, 1)

                def unit(t):
                    scores(t)
                    if t > 0:
                        outputs(t - 1)

                def to_rows():
                    outputs(7)
                    s_oe.wait(pe, i, 4)
                    s_sc.wait(pe, i, 8)
                    for b in range(B):
                        for h in range(2):
                            last = nc.tensor.transpose(sbank[:, b // 2, (b % 2) * 256 + h * P:(b % 2) * 256 + (h + 1) * P],
                                                       ot[:, h, b * P:(b + 1) * P], ident[:])
                    last.then_inc(s_on.sem, 1)

                def to_columns():
                    s_onn.wait(pe, i, 1)
                    for h in range(2):
                        for b in range(B):
                            last = nc.tensor.transpose(sbank[:, 2 + h, b * P:(b + 1) * P],
                                                       oc[:, b * D + h * P:b * D + (h + 1) * P], ident[:])
                    last.then_inc(s_ont.sem, 1)

                def project():
                    s_ogh.wait(pe, i, 2)
                    s_ogl.wait(pe, i, 2)
                    for b in range(B):
                        n = 0
                        for lhs, rhs in ((ogh, wh), (ogh, wl), (ogl, wh)):
                            for h in range(2):
                                last = mm(sbank[:, b // 2, (b % 2) * 256:(b % 2 + 1) * 256], lhs[:, h, b * P:(b + 1) * P],
                                          rhs[:, 4, h, :], start=n == 0, stop=n == 5)
                                n += 1
                    last.then_inc(s_wo.sem, 1)
                return [lambda t=t: unit(t) for t in range(8)] + [to_rows, to_columns, project]
            run_pieces(pe, a_pieces, b_pieces)


def routing(nc, a, sb_, sem_, ident, logits, wts, slots, ids, eid, w1h, w1l, w2h, w2l, brow, ones3):
    ctx = ExitStack()
    with ctx:
        def sb(name, shape, dt=F32):
            return sb_(name, shape, dt, ctx)

        def sem(name):
            return sem_(name, ctx)

        prob = sb("prob", [P, NT, E])
        work = sb("work", [P, NT, E])
        pick = [sb(f"pick{n}", [P, NT, E]) for n in range(2)]
        scan = [sb(f"scan{n}", [P, NT, E]) for n in range(2)]
        top = sb("top", [P, 2, NT])
        col = sb("col", [P, NT])
        both = sb("both", [P, NT, E], F16)
        tri32 = sb("tri32", [P, P])
        tri = sb("tri", [P, P], F16)
        ones = sb("ones", [P, P], F16)
        desc = sb("desc", [P, E])
        ends = sb("ends", [P, E])
        nti = sb("nti", [P, E], I32)
        ntf = sb("ntf", [P, E])
        base = sb("base", [P, E])
        one16 = sb("one16", [P, E])
        jt = sb("jt", [P, SLOT_TILES])
        jti = sb("jti", [P, SLOT_TILES], I32)
        cmpj = sb("cmpj", [P, SLOT_TILES, E])
        low = sb("low", [P, 2 * NT], I32)
        where = sb("where", [P, 2, NT], I32)
        tok = sb("tok", [P, NT], I32)
        zero = sb("zero", [P, SLOT_TILES], I32)
        wcol = sb("wcol", [P, 2, 8], I32)
        tcol = sb("tcol", [P, 8], I32)
        stage = [sb(f"stage{n}", [P, 4 * D]) for n in range(2)]
        bf = sb("bf", [E, 2 * D])
        bparts = [sb(f"bpart{n}", [E, 2 * D], F16) for n in range(3)]
        bank = ctx.enter_context(nc.psum_tensor("rank_bank", [P, 4, 512], F32))

        r_const, r_iota, r_exp, r_max, r_mask, r_rank, r_slot = (sem(s) for s in (
            "r_const", "r_iota", "r_exp", "r_max", "r_mask", "r_rank", "r_slot"))
        zeroed, scattered, id_in, copied = (sem(s) for s in ("zeroed", "scattered", "id_in", "copied"))
        w_in = [sem(f"w_in{n}") for n in range(2)]
        w_hi, w_lo, b_in, b_ok, b_out = (sem(s) for s in ("w_hi", "w_lo", "b_in", "b_ok", "b_out"))
        ch, passed = sem("chain_r"), sem("passed_r")
        NC = 2 * E // 2

        def chunk(m):
            src = a["w1"] if m < NC // 2 else a["w2"]
            hi, lo = (w1h, w1l) if m < NC // 2 else (w2h, w2l)
            k = m % (NC // 2)
            return src[:, 2 * k:2 * k + 2], [t[:, 2 * k:2 * k + 2].rearrange("p e h n -> p (e h n)") for t in (hi, lo)]

        with nc.Block() as block:
            @block.sync
            def _(sp):
                sp.dma_start(tri32[:], a["tri"]).then_inc(r_const, 16)
                sp.dma_start(desc[:], a["desc"]).then_inc(r_const, 16)
                sp.dma_start(bf[:].rearrange("e (k n) -> e k n", k=2), a["b12"]).then_inc(b_in, 16)
                for m in range(NC):
                    if m >= 2:
                        sp.wait_ge(w_lo, m - 1)
                    sp.dma_start(stage[m % 2][:].rearrange("p (e h n) -> p e h n", e=2, h=2), chunk(m)[0]).then_inc(w_in[m % 2], 16)
                sp.wait_ge(b_ok, 5)
                for n in range(3):
                    for k in range(2):
                        sp.dma_start(brow[n:n + 1, k, :, :], bparts[n][:, k * D:(k + 1) * D]).then_inc(b_out, 16)
                sp.wait_ge(b_out, 6 * 16)
                sp.wait_ge(r_iota, 5)
                sp.dma_start(a["slot_ids"].rearrange("(p j) o -> p (j o)", p=P), zero[:]).then_inc(zeroed, 16)
                sp.wait_ge(scattered, 16 * 2 * NT)
                sp.dma_start(ids[:], a["slot_ids"].rearrange("(p j) o -> p (j o)", p=P)).then_inc(id_in, 16)
                sp.wait_ge(id_in, 16)

            @block.scalar
            def _(act):
                act.wait_ge(r_max, 1)
                act.activation(work[:], work[:], ACT.Exp).then_inc(r_exp, 1)
                for m in range(NC):
                    act.wait_ge(w_in[m % 2], 16 * (m // 2 + 1))
                    act.activation(chunk(m)[1][0], stage[m % 2][:], ACT.Copy, scale=SCALE_W).then_inc(w_hi, 1)

            @block.vector
            def _(dve):
                c = Chain(dve, ch, 0)
                link, v = c.link, nc.vector

                def wide(t):
                    return t[:, :, None].to_broadcast([P, NT, E])

                def per_expert(t):
                    return t[:, None, :].to_broadcast([P, NT, E])
                link(v.reduce_max(col[:], logits[:], axis=X))
                v.tensor_tensor(work[:], logits[:], wide(col), ALU.subtract).then_inc(r_max, 1)
                dve.wait_ge(r_exp, 1)
                link(v.reduce_sum(col[:], work[:], axis=X))
                link(v.reciprocal(col[:], col[:]))
                link(v.tensor_tensor(prob[:], work[:], wide(col), ALU.mult))
                dve.wait_ge(r_const, 32)
                for s in range(2):
                    link(v.reduce_max(top[:, s, :], prob[:], axis=X))
                    link(v.tensor_tensor(work[:], prob[:], wide(top[:, s, :]), ALU.is_equal))
                    link(v.tensor_tensor(work[:], work[:], per_expert(desc), ALU.mult))
                    link(v.reduce_max(col[:], work[:], axis=X))
                    link(v.tensor_tensor(pick[s][:], per_expert(desc), wide(col), ALU.is_equal))
                    if s == 0:
                        link(v.scalar_tensor_tensor(out=prob[:], in0=pick[0][:], scalar=-2.0, in1=prob[:], op0=ALU.mult, op1=ALU.add))
                link(v.tensor_tensor(col[:], top[:, 0, :], top[:, 1, :], ALU.add))
                link(v.tensor_scalar(col[:], col[:], 1e-9, None, ALU.max))
                link(v.reciprocal(col[:], col[:]))
                link(v.tensor_tensor(wts[:], top[:], col[:, None, :].to_broadcast([P, 2, NT]), ALU.mult))
                link(v.tensor_tensor(both[:], pick[0][:], pick[1][:], ALU.add))
                link(v.memset(ones[:], 1.0))
                link(v.memset(ones3[:], 1.0))
                link(v.memset(one16[:], 1.0))
                v.tensor_copy(tri[:], tri32[:]).then_inc(r_mask, 1)
                dve.wait_ge(b_in, 16)
                link(v.tensor_scalar(bf[:], bf[:], SCALE_W, None, ALU.mult))
                for n in range(3):
                    v.tensor_copy(bparts[n][:], bf[:]).then_inc(b_ok, 1)
                    dve.wait_ge(b_ok, 2 * n + 1)
                    if n < 2:
                        v.tensor_tensor(bf[:], bf[:], bparts[n][:], ALU.subtract).then_inc(b_ok, 1)
                        dve.wait_ge(b_ok, 2 * n + 2)
                dve.wait_ge(r_rank, 1)
                link(v.tensor_copy(scan[0][:].rearrange("p t e -> p (t e)"), bank[:, 2:4, :].rearrange("p k n -> p (k n)")))
                link(v.tensor_copy(work[:], scan[0][:]))
                s, d = 0, 1
                while d < NT:
                    link(v.tensor_tensor(scan[1 - s][:, d:, :], scan[s][:, d:, :], scan[s][:, :NT - d, :], ALU.add))
                    link(v.tensor_copy(scan[1 - s][:, :d, :], scan[s][:, :d, :]))
                    s, d = 1 - s, 2 * d
                total = scan[s][:, NT - 1, :]
                link(v.tensor_scalar(nti[:], total, float(P - 1), None, ALU.add))
                link(v.tensor_scalar(nti[:], nti[:], 7, None, ALU.arith_shift_right))
                link(v.tensor_copy(ntf[:], nti[:]))
                link(v.tensor_tensor_scan(out=ends[:], data0=one16[:], data1=ntf[:], initial=0.0, op0=ALU.mult, op1=ALU.add))
                link(v.tensor_tensor(base[:], ends[:], ntf[:], ALU.subtract))
                link(v.tensor_scalar(base[:], base[:], float(P), None, ALU.mult))
                off = scan[1 - s]
                link(v.tensor_tensor(off[:], scan[s][:], work[:], ALU.subtract))
                link(v.tensor_tensor(off[:], off[:], per_expert(base), ALU.add))
                link(v.tensor_tensor(off[:].rearrange("p t e -> p (t e)"), off[:].rearrange("p t e -> p (t e)"),
                                     bank[:, 0:2, :].rearrange("p k n -> p (k n)"), ALU.add))
                for s in range(2):
                    link(v.tensor_tensor(work[:], pick[s][:], off[:], ALU.mult))
                    link(v.reduce_sum(col[:], work[:], axis=X))
                    link(v.tensor_copy(slots[:, s, :], col[:]))
                sl = slots[:].rearrange("p s t -> p (s t)")
                wh_ = where[:].rearrange("p s t -> p (s t)")
                link(v.tensor_scalar(low[:], sl, P - 1, None, ALU.bitwise_and))
                link(v.tensor_scalar(wh_, sl, 7, None, ALU.arith_shift_right))
                v.scalar_tensor_tensor(out=wh_, in0=low[:], scalar=float(SLOT_TILES), in1=wh_,
                                       op0=ALU.mult, op1=ALU.add).then_inc(r_slot, 1)
                dve.wait_ge(r_iota, 5)
                link(v.tensor_copy(jt[:], jti[:]))
                link(v.tensor_tensor(cmpj[:], ends[:, None, :].to_broadcast([P, SLOT_TILES, E]),
                                     jt[:, :, None].to_broadcast([P, SLOT_TILES, E]), ALU.is_le))
                link(v.reduce_sum(jt[:], cmpj[:], axis=X))
                link(v.tensor_scalar(eid[:], jt[:], float(E - 1), None, ALU.min))
                for m in range(NC):
                    dve.wait_ge(w_hi, m + 1)
                    hi, lo = chunk(m)[1]
                    v.scalar_tensor_tensor(out=lo, in0=stage[m % 2][:], scalar=SCALE_W, in1=hi,
                                           op0=ALU.mult, op1=ALU.subtract).then_inc(w_lo, 1)

            @block.tensor
            def _(pe):
                pe.wait_ge(r_mask, 1)
                for n, lhs in enumerate((tri, ones)):
                    for k in range(2):
                        last = nc.tensor.matmul(bank[:, 2 * n + k, :], lhs[:], both[:, 32 * k:32 * k + 32, :].rearrange("p t e -> p (t e)"),
                                                start=True, stop=True)
                last.then_inc(r_rank, 1)

            @block.gpsimd
            def _(pool):
                pool.iota(tok[:], [[P, NCH], [L, B]], base=0, channel_multiplier=1).then_inc(r_iota, 1)
                pool.iota(jti[:], [[1, SLOT_TILES]], base=0, channel_multiplier=0).then_inc(r_iota, 1)
                pool.memset(zero[:], 0).then_inc(r_iota, 1)
                pool.memset(wcol[:], 0).then_inc(r_iota, 1)
                pool.memset(tcol[:], 0).then_inc(r_iota, 1)
                pool.wait_ge(r_iota, 5)
                pool.wait_ge(zeroed, 16)
                pool.wait_ge(r_slot, 1)
                with pool.Fori(0, NT // 8, 1) as g:
                    pool.tensor_copy(wcol[:], where[:, :, bass.ds(g * 8, 8)]).then_inc(copied, 1)
                    pool.tensor_copy(tcol[:], tok[:, bass.ds(g * 8, 8)]).then_inc(copied, 1)
                    pool.wait_ge(copied, g * 2 + 2)
                    apart(pool, passed)
                    for k in range(8):
                        for s in range(2):
                            pool.indirect_dma_start(out=a["slot_ids"], out_offset=bass.IndirectOffsetOnAxis(ap=wcol[:, s, k:k + 1], axis=0),
                                                    in_=tcol[:, k:k + 1], in_offset=None).then_inc(scattered, 16)
                    pool.wait_ge(scattered, g * 256 + 256)


def experts(nc, a, sb_, sem_, ident, ids, eid, w1h, w1l, w2h, w2l, brow, ones3):
    ctx = ExitStack()
    with ctx:
        def sb(name, shape, dt=F32):
            return sb_(name, shape, dt, ctx)

        def sem(name):
            return sem_(name, ctx)

        NU = SLOT_TILES // 2
        ic = [sb(f"ic{n}", [P, 2], I32) for n in range(2)]
        xg = [sb(f"xg{n}", [P, 2, D]) for n in range(2)]
        xth = [sb(f"xth{n}", [P, 2, 2, P], F16) for n in range(2)]
        xtl = [sb(f"xtl{n}", [P, 2, 2, P], F16) for n in range(2)]
        st = [sb(f"st{n}", [P, 2, 6]) for n in range(2)]
        mv = [sb(f"mv{n}", [P, 2, 2]) for n in range(2)]
        vr = [sb(f"vr{n}", [P, 2]) for n in range(2)]
        tt = [sb(f"tt{n}", [P, 2]) for n in range(2)]
        gi = [sb(f"gi{n}", [P, 2], I32) for n in range(2)]
        rs = [sb(f"rs{n}", [P, 2]) for n in range(2)]
        nb = [sb(f"nb{n}", [P, 2]) for n in range(2)]
        hn = [sb(f"hn{n}", [P, 2, HID]) for n in range(2)]
        gl = [sb(f"gl{n}", [P, 2, 2, P]) for n in range(2)]
        glh = [sb(f"glh{n}", [P, 2, 2, P], F16) for n in range(2)]
        gll = [sb(f"gll{n}", [P, 2, 2, P], F16) for n in range(2)]
        ys = [sb(f"ys{n}", [P, 2, D]) for n in range(2)]
        g1 = sb("g1", [P, 2, E])
        be1 = sb("be1", [P, 2, E])

        def banks(name):
            return [ctx.enter_context(nc.psum_tensor(f"{name}{n}", [P, 512], F32)) for n in range(2)]
        xb, hb, tb, yb = banks("xb"), banks("hb"), banks("tb"), banks("yb")

        def sig(name, per):
            return Signal(sem(name), per)
        const = sem("f_const")
        f_ic, f_xt, f_xh, f_xl, f_h = sig("f_ic", 1), sig("f_xt", 1), sig("f_xh", 1), sig("f_xl", 1), sig("f_h", 1)
        f_in = [sem(f"f_in{n}") for n in range(2)]
        f_out = [sem(f"f_out{n}") for n in range(2)]
        f_rs, f_hn, f_ht, f_gl, f_glh, f_gll, f_y, f_ys = (
            sig("f_rs", 1), sig("f_hn", 2), sig("f_ht", 1), sig("f_gl", 4), sig("f_glh", 1), sig("f_gll", 1),
            sig("f_y", 1), sig("f_ys", 1))
        ch, passed = sem("chain_f"), sem("passed_f")

        def run(eng, stages):
            last_lag = max(lag for lag, _ in stages)

            def step(s, par, static):
                for lag, f in stages:
                    if static and not 0 <= s - lag < NU:
                        continue
                    f(s - lag, (par - lag) % 2)
            first = last_lag + last_lag % 2 + 2
            for s in range(first):
                step(s, s % 2, True)
            with eng.Fori(first // 2, NU // 2) as k:
                step(k * 2, 0, False)
                step(k * 2 + 1, 1, False)
            for s in range(NU, NU + last_lag):
                step(s, s % 2, True)

        with nc.Block() as block:
            @block.sync
            def _(sp):
                sp.dma_start(g1[:], a["g1"]).then_inc(const, 16)
                sp.dma_start(be1[:], a["be1"]).then_inc(const, 16)

                def store(u, par):
                    f_ys.wait(sp, u, 1)
                    apart(sp, passed)
                    sp.dma_start(a["y_rows"][bass.ds(u * 256, 256), :].rearrange("(k p) c -> p k c", p=P), ys[par][:]).then_inc(f_out[par], 16)
                run(sp, [(3, store)])
                for n in range(2):
                    sp.wait_ge(f_out[n], NU // 2 * 16)

            @block.gpsimd
            def _(pool):
                def gather(u, par):
                    f_xt.wait_before(pool, u, 2, 1)
                    pool.tensor_copy(ic[par][:], ids[:, bass.ds(u * 2, 2)]).then_inc(f_ic.sem, 1)
                    f_ic.wait(pool, u, 1)
                    apart(pool, passed)
                    for k in range(2):
                        pool.indirect_dma_start(out=xg[par][:, k, :], out_offset=None, in_=a["xn_rows"].rearrange("b l c -> (b l) c"),
                                                in_offset=bass.IndirectOffsetOnAxis(ap=ic[par][:, k:k + 1], axis=0)).then_inc(f_in[par], 16)
                run(pool, [(0, gather)])

            @block.tensor
            def _(pe):
                mm = nc.tensor.matmul

                def flip(u, par):
                    pe.wait_ge(f_in[par], after(u, par, 32))
                    f_xl.wait_before(pe, u, 2, 1)
                    for k in range(2):
                        for h in range(2):
                            last = nc.tensor.transpose(xb[par][:, (2 * k + h) * P:(2 * k + h + 1) * P], xg[par][:, k, h * P:(h + 1) * P], ident[:])
                    last.then_inc(f_xt.sem, 1)

                def product(u, par, out, hi, lo, wh, wl, which):
                    for k in range(2):
                        e = pe.value_load(eid[0:1, bass.ds(u * 2 + k, 1)], min_val=0, max_val=E - 1)
                        o = out[par][:, k * 256:(k + 1) * 256]
                        for h in range(2):
                            mm(o, hi[par][:, k, h, :], wh[:, bass.ds(e, 1), h, :].rearrange("p e n -> p (e n)"), start=h == 0, stop=False)
                            mm(o, hi[par][:, k, h, :], wl[:, bass.ds(e, 1), h, :].rearrange("p e n -> p (e n)"), start=False, stop=False)
                            mm(o, lo[par][:, k, h, :], wh[:, bass.ds(e, 1), h, :].rearrange("p e n -> p (e n)"), start=False, stop=False)
                        last = mm(o, ones3[:], brow[0:3, which, bass.ds(e, 1), :].rearrange("p e n -> p (e n)"), start=False, stop=True)
                    return last

                def first(u, par):
                    f_xl.wait(pe, u, 1)
                    f_hn.wait_before(pe, u, 2, 2)
                    product(u, par, hb, xth, xtl, w1h, w1l, 0).then_inc(f_h.sem, 1)

                def flip_back(u, par):
                    f_hn.wait(pe, u, 2)
                    f_gl.wait_before(pe, u, 2, 4)
                    for k in range(2):
                        for h in range(2):
                            last = nc.tensor.transpose(tb[par][:, (2 * k + h) * P:(2 * k + h + 1) * P], hn[par][:, k, h * P:(h + 1) * P], ident[:])
                    last.then_inc(f_ht.sem, 1)

                def second(u, par):
                    f_glh.wait(pe, u, 1)
                    f_gll.wait(pe, u, 1)
                    f_ys.wait_before(pe, u, 2, 1)
                    product(u, par, yb, glh, gll, w2h, w2l, 1).then_inc(f_y.sem, 1)
                run(pe, [(0, flip), (1, first), (2, flip_back), (3, second)])

            @block.scalar
            def _(act):
                act.wait_ge(const, 32)

                def high(u, par):
                    f_xt.wait(act, u, 1)
                    f_h.wait_before(act, u, 2, 1)
                    act.activation(xth[par][:].rearrange("p k h s -> p (k h s)"), xb[par][:], ACT.Copy).then_inc(f_xh.sem, 1)

                def norm(u, par):
                    f_rs.wait(act, u, 1)
                    f_ht.wait_before(act, u, 2, 1)
                    for k in range(2):
                        act.activation(hn[par][:, k, :], hb[par][:, k * 256:(k + 1) * 256], ACT.Identity, scale=rs[par][:, k:k + 1],
                                       bias=nb[par][:, k:k + 1]).then_inc(f_hn.sem, 1)

                def gelu(u, par):
                    f_ht.wait(act, u, 1)
                    f_gll.wait_before(act, u, 2, 1)
                    for k in range(2):
                        e = act.value_load(eid[0:1, bass.ds(u * 2 + k, 1)], min_val=0, max_val=E - 1)
                        for h in range(2):
                            act.activation(gl[par][:, k, h, :], tb[par][:, (2 * k + h) * P:(2 * k + h + 1) * P], ACT.Gelu,
                                           scale=g1[:, h, bass.ds(e, 1)], bias=be1[:, h, bass.ds(e, 1)]).then_inc(f_gl.sem, 1)

                def out(u, par):
                    f_y.wait(act, u, 1)
                    act.wait_ge(f_out[par], after(u, par, 16) - 16)
                    act.activation(ys[par][:].rearrange("p k c -> p (k c)"), yb[par][:], ACT.Copy, scale=UNSCALE).then_inc(f_ys.sem, 1)
                run(act, [(0, high), (1, norm), (2, gelu), (3, out)])

            @block.vector
            def _(dve):
                c = Chain(dve, ch, LINKS_F, passed)

                def low(u, par):
                    f_xh.wait(dve, u, 1)
                    f_h.wait_before(dve, u, 2, 1)
                    nc.vector.tensor_tensor(xtl[par][:].rearrange("p k h s -> p (k h s)"), xb[par][:],
                                            xth[par][:].rearrange("p k h s -> p (k h s)"), ALU.subtract).then_inc(f_xl.sem, 1)

                def moments(u, par):
                    c.start(u)
                    f_h.wait(dve, u, 1)
                    f_hn.wait_before(dve, u, 2, 2)
                    for k in range(2):
                        c.link(nc.vector.bn_stats(st[par][:, k, :], hb[par][:, k * 256:(k + 1) * 256]), True)
                    for k in range(2):
                        c.link(nc.vector.bn_aggr(mv[par][:, k, :], st[par][:, k, :]), True)
                    c.link(nc.vector.tensor_scalar(vr[par][:], mv[par][:, :, 1], EPS * SCALE_W * SCALE_W, None, ALU.add))
                    inverse_sqrt(nc, c, rs[par][:], vr[par][:], tt[par][:], gi[par][:])
                    nc.vector.scalar_tensor_tensor(out=nb[par][:], in0=mv[par][:, :, 0], scalar=-1.0, in1=rs[par][:],
                                                   op0=ALU.mult, op1=ALU.mult).then_inc(f_rs.sem, 1)
                    c.end()

                def halves(u, par):
                    f_gl.wait(dve, u, 4)
                    f_y.wait_before(dve, u, 2, 1)
                    nc.vector.tensor_copy(glh[par][:], gl[par][:]).then_inc(f_glh.sem, 1)
                    f_glh.wait(dve, u, 1)
                    nc.vector.tensor_tensor(gll[par][:], gl[par][:], glh[par][:], ALU.subtract).then_inc(f_gll.sem, 1)
                run(dve, [(0, low), (1, moments), (2, halves)])


def combine(nc, a, sb_, sem_, wts, slots):
    ctx = ExitStack()
    with ctx:
        def sb(name, shape, dt=F32):
            return sb_(name, shape, dt, ctx)

        def sem(name):
            return sem_(name, ctx)
        xr = [sb(f"xr{n}", [P, B, D]) for n in range(2)]
        ar = [sb(f"ar{n}", [P, B, D]) for n in range(2)]
        yr = [sb(f"yr{n}", [P, 2, B, D]) for n in range(2)]
        sx = [sb(f"sx{n}", [P, 2, B], I32) for n in range(2)]
        wx = [sb(f"wx{n}", [P, 2, B]) for n in range(2)]
        passed = sem("passed_c")
        c_in = [sem(f"c_in{n}") for n in range(2)]
        c_y = [sem(f"c_y{n}") for n in range(2)]
        c_out = [sem(f"c_out{n}") for n in range(2)]

        def sig(name, per):
            return Signal(sem(name), per)
        c_idx, c_w, c_sum, c_one, c_two = sig("c_idx", 1), sig("c_w", 1), sig("c_sum", 1), sig("c_one", 4), sig("c_two", 4)

        def run(eng, f):
            for i in range(2):
                f(i, i)
            with eng.Fori(1, NCH // 2) as k:
                f(k * 2, 0)
                f(k * 2 + 1, 1)

        def rows(name, i):
            return a[name][:, bass.ds(i * P, P), :].rearrange("b t c -> t b c")

        with nc.Block() as block:
            @block.sync
            def _(sp):
                def load(i, par):
                    c_two.wait_before(sp, i, 2, 4)
                    apart(sp, passed)
                    sp.wait_ge(c_out[par], after(i, par, 16) - 16)
                    apart(sp, passed)
                    sp.dma_start(xr[par][:], rows("x", i)).then_inc(c_in[par], 16)
                    sp.dma_start(ar[par][:], rows("attn_rows", i)).then_inc(c_in[par], 16)
                run(sp, load)
                for n in range(2):
                    sp.wait_ge(c_out[n], NCH // 2 * 16)

            @block.scalar
            def _(act):
                def store(i, par):
                    c_two.wait(act, i, 4)
                    act.dma_start(rows("out", i), xr[par][:]).then_inc(c_out[par], 16)
                run(act, store)

            @block.gpsimd
            def _(pool):
                def gather(i, par):
                    c_two.wait_before(pool, i, 2, 4)
                    if isinstance(i, int) and i < 2:
                        pass
                    else:
                        pool.wait_ge(c_y[par], after(i, par, 128) - 128)
                    pool.tensor_copy(sx[par][:], slots[:, :, bass.ds(i * B, B)]).then_inc(c_idx.sem, 1)
                    c_idx.wait(pool, i, 1)
                    apart(pool, passed)
                    for s in range(2):
                        for b in range(B):
                            pool.indirect_dma_start(out=yr[par][:, s, b, :], out_offset=None, in_=a["y_rows"],
                                                    in_offset=bass.IndirectOffsetOnAxis(ap=sx[par][:, s, b:b + 1], axis=0)).then_inc(c_y[par], 16)
                run(pool, gather)

            @block.vector
            def _(dve):
                v = nc.vector

                def add(i, par):
                    dve.wait_ge(c_in[par], after(i, par, 32))
                    v.tensor_tensor(xr[par][:], xr[par][:], ar[par][:], ALU.add).then_inc(c_sum.sem, 1)
                    v.tensor_copy(wx[par][:], wts[:, :, bass.ds(i * B, B)]).then_inc(c_w.sem, 1)
                    c_sum.wait(dve, i, 1)
                    c_w.wait(dve, i, 1)
                    dve.wait_ge(c_y[par], after(i, par, 128))
                    for b in range(B):
                        v.scalar_tensor_tensor(out=xr[par][:, b, :], in0=yr[par][:, 0, b, :], scalar=wx[par][:, 0, b:b + 1],
                                               in1=xr[par][:, b, :], op0=ALU.mult, op1=ALU.add).then_inc(c_one.sem, 1)
                    for b in range(B):
                        c_one.wait(dve, i, b + 1)
                        v.scalar_tensor_tensor(out=xr[par][:, b, :], in0=yr[par][:, 1, b, :], scalar=wx[par][:, 1, b:b + 1],
                                               in1=xr[par][:, b, :], op0=ALU.mult, op1=ALU.add).then_inc(c_two.sem, 1)
                run(dve, add)

def layouts(i):
    import numpy as np
    f = lambda n: np.asarray(i[n])
    rows = lambda w: w.reshape(2, P, -1).transpose(1, 0, 2)
    p, s = np.arange(P)[:, None], np.arange(P)[None, :]
    key, t = np.arange(P)[:, None] % 64, np.arange(64)[None, :]
    causal = (t >= key).astype(np.float32)
    winit = np.zeros((P, B, 2, P), np.float32)
    for h in range(H):
        r = DK * (h % 8)
        winit[r:r + DK, :, h // 8, r:r + DK] = f("L0_attn_W_init")[0, h][:, None, :]
    a = {
        "x": f("L0_attn_hidden_states"),
        "wat": np.stack([rows(f(f"L0_attn_W{m}").T) for m in "qkvgo"]),
        "wr": rows(f("L0_ffn_Wr")),
        "br": np.broadcast_to(f("L0_ffn_br"), (P, E)),
        "taps": np.stack([f(f"L0_attn_conv_{m}").reshape(2, P, 4) for m in "qkv"]).reshape(6, P, 4).transpose(1, 0, 2),
        "gam": np.tile(f("L0_attn_ln_gamma"), P // DK)[:, None],
        "bet": np.tile(f("L0_attn_ln_beta"), P // DK)[:, None],
        "winit": winit,
        "ident": np.eye(P, dtype=np.float32),
        "cmask": np.concatenate([causal, np.ones((P, 64), np.float32), causal], 1),
        "bdmask": (p // DK == s // DK).astype(np.float32),
        "tri": (p < s).astype(np.float32),
        "desc": np.broadcast_to(E - np.arange(E, dtype=np.float32), (P, E)),
        "w1": f("L0_ffn_W1").reshape(E, 2, P, HID).transpose(2, 0, 1, 3),
        "w2": f("L0_ffn_W2").reshape(E, 2, P, D).transpose(2, 0, 1, 3),
        "b12": np.stack([f("L0_ffn_b1"), f("L0_ffn_b2")], 1),
        "g1": f("L0_ffn_g1").reshape(E, 2, P).transpose(2, 1, 0),
        "be1": f("L0_ffn_be1").reshape(E, 2, P).transpose(2, 1, 0),
        "parity": (p // DK % 2 == np.arange(2)[None, :]).astype(np.float32),
    }
    return {k: np.ascontiguousarray(v) for k, v in a.items()}


SCRATCH = {"xn_rows": ((B, L, D), F32), "attn_rows": ((B, L, D), F32), "y_rows": ((SLOT_TILES * P, D), F32),
           "slot_ids": ((SLOT_TILES * P, 1), I32)}


def kernel(**inputs):
    import numpy as np
    import concourse.bacc as bacc
    from concourse.bass_utils import run_bass_kernel_spmd

    nc = bacc.Bacc("TRN2", target_bir_lowering=False, num_devices=1)
    arrays = {f"in_{k}": v for k, v in layouts(inputs).items()}
    aps = {k[3:]: nc.dram_tensor(k, v.shape, mybir.dt.from_np(v.dtype), kind="ExternalInput").ap() for k, v in arrays.items()}
    for name, (shape, dtype) in SCRATCH.items():
        aps[name] = nc.dram_tensor(name, shape, dtype, kind="Internal").ap()
    aps["out"] = nc.dram_tensor("out", (B, L, D), F32, kind="ExternalOutput").ap()
    program(nc, aps)
    return run_bass_kernel_spmd(nc, [arrays], core_ids=[0]).results[0]["out"]
```

```python
from contextlib import ExitStack

import concourse.bass as bass
from concourse import mybir

F32 = mybir.dt.float32
F16 = mybir.dt.float16
I32 = mybir.dt.int32
ALU = mybir.AluOpType
ACT = mybir.ActivationFunctionType
X = mybir.AxisListType.X

P = 128
B, L, D = 4, 2048, 256
H, DK = 16, 16
NCH = L // P
W = B * P
NT = B * NCH
E, HID = 16, 256
SCALE_W = 64.0
UNSCALE = 1.0 / SCALE_W
EPS = 1e-5
EPS_NORM = 1e-12
SLOT_TILES = 144
GRP = 4
MAGIC = 1597463007.0

LINKS_NORM = 20
LINKS_CONV = 12
LINKS_RK = 12
LINKS_B = 17
LINKS_F = 16


class Signal:

    def __init__(self, sem, per):
        self.sem, self.per = sem, per

    def at(self, i, k):
        return i * self.per + k

    def wait(self, eng, i, k):
        eng.wait_ge(self.sem, i * self.per + k)

    def wait_before(self, eng, i, back, k):
        if isinstance(i, int):
            if i - back < 0:
                return
        eng.wait_ge(self.sem, (i - back) * self.per + k if isinstance(i, int) else i * self.per + (k - back * self.per))


def apart(eng, passed):
    eng.sem_inc(passed, 1)


def after(u, par, by):
    return (u // 2 + 1) * by if isinstance(u, int) else u * (by // 2) + (by - par * (by // 2))


class Chain:

    def __init__(self, eng, sem, step, passed=None):
        self.eng, self.sem, self.step, self.i, self.n, self.passed = eng, sem, step, 0, 0, passed

    def start(self, i, n=0):
        self.i, self.n = i, n

    def count(self, ins):
        ins.then_inc(self.sem, 1)
        self.n += 1

    def wait(self, next_apart=False):
        self.eng.wait_ge(self.sem, self.i * self.step + self.n)
        if next_apart:
            apart(self.eng, self.passed)

    def link(self, ins):
        self.count(ins)
        self.wait()

    def end(self):
        assert self.n == self.step, f"{self.sem}: {self.n} links, not {self.step}"


def inverse_sqrt(nc, chain, y, x, t, guess):
    chain.link(nc.vector.tensor_scalar(guess, x.bitcast(I32), 1, None, ALU.arith_shift_right))
    chain.link(nc.vector.tensor_scalar(guess, guess, -1.0, MAGIC, ALU.mult, ALU.add))
    src = guess.bitcast(F32)
    for _ in range(3):
        chain.link(nc.vector.tensor_tensor(t, src, src, ALU.mult))
        chain.link(nc.vector.scalar_tensor_tensor(out=t, in0=t, scalar=-0.5, in1=x, op0=ALU.mult, op1=ALU.mult))
        chain.link(nc.vector.scalar_tensor_tensor(out=y, in0=t, scalar=1.5, in1=src, op0=ALU.add, op1=ALU.mult))
        src = y


def program(nc, a, debug=False):
    x_d, out_d = a["x"], a["out"]
    xn_d, attn_d = a["xn_rows"], a["attn_rows"]
    ctx = ExitStack()
    with ctx:
        def sb(name, shape, dt=F32, c=ctx):
            return c.enter_context(nc.sbuf_tensor(name, shape, dt))

        def sem(name, c=ctx):
            return c.enter_context(nc.semaphore(name))

        ident = sb("ident", [P, P])
        logits = sb("logits", [P, NT, E])

        wts = sb("wts", [P, 2, NT])
        slots = sb("slots", [P, 2, NT], I32)
        attention(nc, a, sb, sem, ident, logits)
        mid = ExitStack()
        with mid:
            ids = sb("ids", [P, SLOT_TILES], I32, mid)
            eid = sb("eid", [P, SLOT_TILES], I32, mid)
            w1h, w1l = sb("w1h", [P, E, 2, HID], F16, mid), sb("w1l", [P, E, 2, HID], F16, mid)
            w2h, w2l = sb("w2h", [P, E, 2, D], F16, mid), sb("w2l", [P, E, 2, D], F16, mid)
            brow = sb("brow", [3, 2, E, D], F16, mid)
            ones3 = sb("ones3", [3, P], F16, mid)
            kept = (ids, eid, w1h, w1l, w2h, w2l, brow, ones3)
            routing(nc, a, sb, sem, ident, logits, wts, slots, *kept)
            experts(nc, a, sb, sem, ident, *kept)
        combine(nc, a, sb, sem, wts, slots)


def attention(nc, a, sb_, sem_, ident, logits):
    ctx = ExitStack()
    with ctx:
        def sb(name, shape, dt=F32):
            return sb_(name, shape, dt, ctx)

        def sem(name):
            return sem_(name, ctx)

        wh = sb("wh", [P, 5, 2, D], F16)
        wl = sb("wl", [P, 5, 2, D], F16)
        rh = sb("rh", [P, 2, E], F16)
        rl = sb("rl", [P, 2, E], F16)
        taps = sb("taps", [P, 6, 4])
        gam = sb("gam", [P, 1])
        bet = sb("bet", [P, 1])
        br = sb("br", [P, E])
        cmask = sb("cmask", [P, 192])
        bdmask = sb("bdmask", [P, P])
        parity = sb("parity", [P, 2])
        state = sb("state", [P, B, 2, P])

        xs = sb("xs", [P, B, D])
        stats = sb("stats", [P, B, 6])
        mv = sb("mv", [P, B, 2])
        rstd = sb("rstd", [P, B])
        nbias = sb("nbias", [P, B])
        tn = sb("tn", [P, 2 * B])
        gn = sb("gn", [P, B], I32)
        xn = sb("xn", [P, B, D])
        xh = sb("xh", [P, 2, W], F16)
        xl = sb("xl", [P, 2, W], F16)
        pre = sb("pre", [P, 6, B, P + 3])
        acc = sb("acc", [P, 2, W])
        kt = sb("kt", [P, 2, W])
        vt = sb("vt", [P, 2, W])
        khf = sb("khf", [P, 2, W], F16)
        klf = sb("klf", [P, 2, W], F16)
        sq = sb("sq", [P, 2, W])
        ssq = sb("ssq", [P, B, 32])
        rk = sb("rk", [P, B * H])
        ta = sb("ta", [P, B * H])
        ga = sb("ga", [P, B * H], I32)
        qt = [sb(f"qt{n}", [P, 2, W]) for n in range(2)]
        qh = [sb(f"qh{n}", [P, 2, W], F16) for n in range(2)]
        ql = [sb(f"ql{n}", [P, 2, W], F16) for n in range(2)]
        kmh = [sb(f"kmh{n}", [P, 2, 8, 2, 64], F16) for n in range(2)]
        kml = [sb(f"kml{n}", [P, 2, 8, 2, 64], F16) for n in range(2)]
        gate = [sb(f"gate{n}", [P, 2, W]) for n in range(2)]
        kn = [sb(f"kn{n}", [P, B, D]) for n in range(2)]
        vp = [sb(f"vp{n}", [P, B, D]) for n in range(2)]
        vbd = [sb(f"vbd{n}", [P, B, 2, 8, 32]) for n in range(2)]
        epsq = [sb(f"epsq{n}", [P, B * H]) for n in range(2)]
        sc = [sb(f"sc{n}", [P, 4, 192]) for n in range(2)]
        um = [sb(f"um{n}", [P, 2, P]) for n in range(2)]
        ot = sb("ot", [P, 2, W])
        osum = sb("osum", [P, B * H])
        oc = sb("oc", [P, B * D])
        osq = sb("osq", [P, B * D])
        ro = sb("ro", [P, B * H])
        tb = sb("tb", [P, B * H])
        gb = sb("gb", [P, B * H], I32)
        og = sb("og", [P, 2, W])
        ogh = sb("ogh", [P, 2, W], F16)
        ogl = sb("ogl", [P, 2, W], F16)
        at = sb("at", [P, B, D])

        banks = [ctx.enter_context(nc.psum_tensor(f"bank{n}", [P, W], F32)) for n in range(3)]
        sbank = ctx.enter_context(nc.psum_tensor("sbank", [P, 4, W], F32))
        oubank = ctx.enter_context(nc.psum_tensor("oubank", [P, W], F32))

        loaded, loaded_r, split_h, split_l, ready = (sem(s) for s in ("loaded", "loaded_r", "split_h", "split_l", "ready"))
        loaded_w = [sem(f"loaded_w{n}") for n in range(2)]
        wf = [osq, oc]
        wide = [a["wat"][m] for m in range(5)]

        with nc.Block() as block:
            @block.sync
            def _(sp):
                for dst, src in ((ident, "ident"), (taps, "taps"), (gam, "gam"), (bet, "bet"), (br, "br"),
                                 (cmask, "cmask"), (bdmask, "bdmask"), (parity, "parity"), (state, "winit")):
                    sp.dma_start(dst[:], a[src]).then_inc(loaded, 16)
                for m in range(5):
                    if m >= 2:
                        sp.wait_ge(split_l, m - 1)
                    sp.dma_start(wf[m % 2][:, 0:512].rearrange("p (h n) -> p h n", h=2), wide[m]).then_inc(loaded_w[m % 2], 16)
                sp.dma_start(sq[:, 0, 0:2 * E].rearrange("p (h n) -> p h n", h=2), a["wr"]).then_inc(loaded_r, 16)
                sp.wait_ge(loaded, 9 * 16)

            @block.scalar
            def _(act):
                for m in range(5):
                    act.wait_ge(loaded_w[m % 2], 16 * (m // 2 + 1))
                    act.activation(wh[:, m, :, :].rearrange("p h n -> p (h n)"), wf[m % 2][:, 0:512], ACT.Copy,
                                   scale=SCALE_W).then_inc(split_h, 1)
                act.wait_ge(loaded_r, 16)
                act.activation(rh[:].rearrange("p h n -> p (h n)"), sq[:, 0, 0:2 * E], ACT.Copy,
                               scale=SCALE_W).then_inc(split_h, 1)

            @block.vector
            def _(dve):
                for m in range(5):
                    dve.wait_ge(split_h, m + 1)
                    dve.wait_ge(loaded_w[m % 2], 16 * (m // 2 + 1))
                    dve.scalar_tensor_tensor(out=wl[:, m, :, :].rearrange("p h n -> p (h n)"), in0=wf[m % 2][:, 0:512],
                                             scalar=SCALE_W, in1=wh[:, m, :, :].rearrange("p h n -> p (h n)"),
                                             op0=ALU.mult, op1=ALU.subtract).then_inc(split_l, 1)
                dve.wait_ge(split_h, 6)
                dve.wait_ge(loaded_r, 16)
                dve.scalar_tensor_tensor(out=rl[:].rearrange("p h n -> p (h n)"), in0=sq[:, 0, 0:2 * E], scalar=SCALE_W,
                                         in1=rh[:].rearrange("p h n -> p (h n)"),
                                         op0=ALU.mult, op1=ALU.subtract).then_inc(split_l, 1)
                dve.wait_ge(loaded, 9 * 16)
                dve.tensor_scalar(taps[:, :, 3], taps[:, :, 3], 1.0, None, ALU.add).then_inc(ready, 1)
                dve.memset(pre[:], 0.0).then_inc(ready, 1)

            @block.gpsimd
            def _(pool):
                for n in range(2):
                    pool.memset(vbd[n][:], 0.0).then_inc(ready, 1)
                pool.wait_ge(ready, 4)

        def sig(name, per):
            return Signal(sem(name), per)

        x_in, xn_out, at_out = sig("x_in", 16), sig("xn_out", 16), sig("at_out", 16)
        s_rstd, s_xn, s_xt, s_xh, s_xl = sig("rstd_ok", 1), sig("xn_ok", 4), sig("xt_ok", 2), sig("xh_ok", 2), sig("xl_ok", 2)
        s_lg, s_lge = sig("logit_mm", 1), sig("logit_ok", 1)
        s_proj, s_p, s_g = sig("proj_mm", 8), sig("pre_ok", 6), sig("gate_ok", 2)
        s_tap, s_conv, s_hist, s_silu = sig("tap_ok", 6), sig("conv_ok", 6), sig("hist_ok", 1), sig("silu_ok", 6)
        s_qkt, s_kn, s_sq, s_ssq = sig("qkt_ok", 4), sig("kn_ok", 4), sig("sq_ok", 4), sig("ssq_ok", 4)
        s_vtt, s_vp, s_vbd, s_epsq = sig("vt_ok", 2), sig("vp_ok", 2), sig("vbd_ok", 4), sig("epsq_ok", 1)
        s_qh, s_ql, s_kh, s_kl, s_km = sig("qh_ok", 2), sig("ql_ok", 2), sig("kh_ok", 2), sig("kl_ok", 2), sig("km_ok", 8)
        s_s, s_sc, s_o, s_oe = sig("score_mm", 8), sig("score_ok", 8), sig("o_mm", 8), sig("o_out", 4)
        s_u, s_um, s_st = sig("u_mm", 4), sig("um_ok", 4), sig("state_ok", 4)
        s_on, s_oc, s_osq, s_onn, s_ont = sig("on_t", 2), sig("oc_ok", 2), sig("osq_ok", 2), sig("onorm_ok", 1), sig("onorm_t", 2)
        s_oga, s_ogg, s_ogh, s_ogl = sig("oga_ok", 2), sig("ogg_ok", 2), sig("ogh_ok", 2), sig("ogl_ok", 2)
        s_wo, s_at = sig("wo_mm", 2), sig("at_ok", 2)
        chain_norm, chain_conv, chain_rk, chain_b, passed = (sem(s) for s in (
            "chain_norm", "chain_conv", "chain_rk", "chain_b", "passed_a"))

        LAST = 28 // 8

        def run_places(eng, pieces):
            slots_ = [[(a // 8, f) for a, f in pieces if a % 8 == k] for k in range(8)]

            def step(s, par, static):
                for slot in slots_:
                    for lag, f in slot:
                        if not static or 0 <= s - lag < NCH:
                            f(s - lag, (par - lag) % 2)
            first = 6
            for s in range(first):
                step(s, s % 2, True)
            with eng.Fori(first // 2, NCH // 2) as k:
                step(k * 2, 0, False)
                step(k * 2 + 1, 1, False)
            for s in range(NCH, NCH + LAST + 1):
                step(s, s % 2, True)

        turns = [("g0", 1, s_g, 1), ("g1", 1, s_g, 2), ("qk0", 1, s_sq, 1), ("qk1", 1, s_sq, 2),
                 ("qk2", 1, s_sq, 3), ("qk3", 1, s_sq, 4), ("x0", 0, s_xl, 1), ("x1", 0, s_xl, 2),
                 ("v0t", 1, s_vp, 1), ("v1t", 1, s_vp, 2), ("route", 0, s_lge, 1), ("p0", 0, s_p, 1),
                 ("wo0", 3, s_at, 1), ("wo1", 3, s_at, 2), ("p1", 0, s_p, 2), ("p2", 0, s_p, 3),
                 ("on0", 2, s_oc, 1), ("on1", 2, s_oc, 2), ("p3", 0, s_p, 4), ("p4", 0, s_p, 5),
                 ("p5", 0, s_p, 6), ("ont0", 2, s_oga, 1), ("ont1", 2, s_oga, 2)]
        place_of = {name: n for n, (name, *_) in enumerate(turns)}

        def bank(name):
            return banks[place_of[name] % 3]

        def wait_bank(eng, name, i):
            n = place_of[name]
            step = i + turns[n][1] if isinstance(i, int) else None
            back = 0
            while True:
                n -= 3
                if n < 0:
                    n, back = {-3: 21, -2: 22, -1: 20}[n], back + 1
                _, lag, signal, k = turns[n]
                off = turns[place_of[name]][1] - lag - back
                if step is None:
                    eng.wait_ge(signal.sem, i * signal.per + (off * signal.per + k))
                    return
                if step - back < 0:
                    return
                if 0 <= i + off < NCH:
                    signal.wait(eng, i + off, k)
                    return

        block = ctx.enter_context(nc.Block())

        @block.sync
        def _(sp):
            def load(i, par):
                s_xn.wait_before(sp, i, 1, 4)
                apart(sp, passed)
                sp.dma_start(xs[:], a["x"][:, bass.ds(i * P, P), :].rearrange("b t c -> t b c")).then_inc(x_in.sem, 16)

            def store_xn(i, par):
                s_xn.wait(sp, i, 4)
                apart(sp, passed)
                sp.dma_start(a["xn_rows"][:, bass.ds(i * P, P), :].rearrange("b t c -> t b c"), xn[:]).then_inc(xn_out.sem, 16)

            def store_at(i, par):
                s_at.wait(sp, i, 2)
                apart(sp, passed)
                sp.dma_start(a["attn_rows"][:, bass.ds(i * P, P), :].rearrange("b t c -> t b c"), at[:]).then_inc(at_out.sem, 16)
            run_places(sp, [(0, load), (1, store_xn), (28, store_at)])
            xn_out.wait(sp, NCH - 1, 16)
            at_out.wait(sp, NCH - 1, 16)

        @block.vector
        def _(dve):
            c_norm, c_conv = Chain(dve, chain_norm, LINKS_NORM, passed), Chain(dve, chain_conv, LINKS_CONV)
            c_rk, c_b = Chain(dve, chain_rk, LINKS_RK), Chain(dve, chain_b, LINKS_B)

            def norm(i, par):
                c_norm.start(i)
                x_in.wait(dve, i, 16)
                s_xn.wait_before(dve, i, 1, 4)
                for b in range(B):
                    c_norm.count(nc.vector.bn_stats(stats[:, b, :], xs[:, b, :]))
                c_norm.wait(True)
                for b in range(B):
                    c_norm.count(nc.vector.bn_aggr(mv[:, b, :], stats[:, b, :]))
                c_norm.wait()
                c_norm.link(nc.vector.tensor_scalar(tn[:, 0:B], mv[:, :, 1], EPS, None, ALU.add))
                inverse_sqrt(nc, c_norm, rstd[:], tn[:, 0:B], tn[:, B:2 * B], gn[:])
                nc.vector.scalar_tensor_tensor(out=nbias[:], in0=mv[:, :, 0], scalar=-1.0, in1=rstd[:],
                                               op0=ALU.mult, op1=ALU.mult).then_inc(s_rstd.sem, 1)
                c_norm.end()

            def low(i, par):
                for h in range(2):
                    s_xh.wait(dve, i, h + 1)
                    nc.vector.tensor_tensor(xl[:, h, :], bank(f"x{h}")[:], xh[:, h, :], ALU.subtract).then_inc(s_xl.sem, 1)

            def logit(i, par):
                s_lg.wait(dve, i, 1)
                nc.vector.scalar_tensor_tensor(
                    out=logits[:, bass.ds(i * B, B), :], in0=bank("route")[:, 0:B * E].rearrange("p (b e) -> p b e", b=B),
                    scalar=UNSCALE, in1=br[:, None, :].to_broadcast([P, B, E]),
                    op0=ALU.mult, op1=ALU.add).then_inc(s_lge.sem, 1)

            def conv(blk):
                def f(i, par):
                    c_conv.start(i, 2 * blk)
                    s_tap.wait(dve, i, blk + 1)
                    c = acc[:, blk % 2, :].rearrange("p (b t) -> p b t", b=B)
                    for j in range(3):
                        ins = nc.vector.scalar_tensor_tensor(out=c, in0=pre[:, blk, :, j:j + P], scalar=taps[:, blk, j:j + 1],
                                                             in1=c, op0=ALU.mult, op1=ALU.add)
                        if j < 2:
                            c_conv.link(ins)
                        else:
                            ins.then_inc(s_conv.sem, 1)
                    if blk == 5:
                        c_conv.end()
                        s_conv.wait(dve, i, 6)
                        nc.vector.tensor_copy(pre[:, :, :, 0:3].rearrange("p k b t -> p (k b) t"),
                                              pre[:, :, :, P:P + 3].rearrange("p k b t -> p (k b) t")).then_inc(s_hist.sem, 1)
                return f

            def masks(i, par):
                for n, (src, dst, ok) in enumerate(((khf, kmh, s_kh), (klf, kml, s_kl))):
                    for o in range(2):
                        ok.wait(dve, i, o + 1)
                        if n == 0 and o == 0:
                            s_s.wait_before(dve, i, 2, 8)
                        for e in range(2):
                            nc.vector.tensor_scalar(dst[par][:, o, :, e, :], src[:, o, :].rearrange("p (k s) -> p k s", s=64),
                                                    parity[:, e:e + 1], None, ALU.mult).then_inc(s_km.sem, 1)

            def sums(bs):
                def f(i, par):
                    for b in bs:
                        s_sq.wait(dve, i, b + 1)
                        nc.vector.reduce_sum(ssq[:, b, :], sq[:, b % 2, :].rearrange("p (h k) -> p h k", k=DK),
                                             axis=X).then_inc(s_ssq.sem, 1)
                return f

            def key_norm(i, par):
                c_rk.start(i)
                s_ssq.wait(dve, i, B)
                s_onn.wait_before(dve, i, 2, 1)
                nc.vector.tensor_scalar(epsq[par][:].rearrange("p (b h) -> p b h", b=B), ssq[:, :, 0:H], EPS_NORM, EPS,
                                        ALU.add, ALU.mult).then_inc(s_epsq.sem, 1)
                c_rk.link(nc.vector.tensor_scalar(ta[:].rearrange("p (b h) -> p b h", b=B), ssq[:, :, H:2 * H], EPS_NORM, None, ALU.add))
                inverse_sqrt(nc, c_rk, rk[:], ta[:], sq[:, 0, 0:B * H], ga[:])
                c_rk.end()

            def values(i, par):
                for n in range(2):
                    s_vtt.wait(dve, i, n + 1)
                    if n == 0:
                        s_u.wait_before(dve, i, 2, 4)
                        s_vbd.wait_before(dve, i, 2, 4)
                    nc.vector.tensor_tensor(vp[par][:, 2 * n:2 * n + 2, :].rearrange("p b (h k) -> p (b h) k", k=DK),
                                            bank(f"v{n}t")[:].rearrange("p (h k) -> p h k", k=DK),
                                            rk[:, 2 * n * H:(2 * n + 2) * H][:, :, None].to_broadcast([P, 2 * H, DK]),
                                            ALU.mult).then_inc(s_vp.sem, 1)

            def mask_scores(t):
                def f(i, par):
                    s_s.wait(dve, i, t + 1)
                    if t < 2:
                        s_o.wait_before(dve, i, 1, 7 + t)
                    else:
                        s_o.wait(dve, i, t - 1)
                    nc.vector.tensor_tensor(sc[t % 2][:], sbank[:, :, 0:192], cmask[:, None, :].to_broadcast([P, 4, 192]),
                                            ALU.mult).then_inc(s_sc.sem, 1)
                return f

            def mask_update(b):
                def f(i, par):
                    s_u.wait(dve, i, b + 1)
                    s_oe.wait(dve, i, b + 1)
                    if b < 2:
                        s_st.wait_before(dve, i, 1, 3 + b)
                    else:
                        s_st.wait(dve, i, b - 1)
                    nc.vector.tensor_tensor(um[b % 2][:], oubank[:, 256:512].rearrange("p (h n) -> p h n", h=2),
                                            bdmask[:, None, :].to_broadcast([P, 2, P]), ALU.mult).then_inc(s_um.sem, 1)
                return f

            def centre(i, par):
                c_b.start(i)
                for n in range(2):
                    s_on.wait(dve, i, n + 1)
                    cols = slice(2 * n * H, (2 * n + 2) * H)
                    full = bank(f"on{n}")[:].rearrange("p (h v) -> p h v", v=DK)
                    c_b.link(nc.vector.reduce_sum(osum[:, cols], full, axis=X))
                    c_b.link(nc.vector.tensor_scalar(osum[:, cols], osum[:, cols], 1.0 / DK, None, ALU.mult))
                    nc.vector.tensor_tensor(oc[:, n * W:(n + 1) * W].rearrange("p (h v) -> p h v", v=DK), full,
                                            osum[:, cols][:, :, None].to_broadcast([P, 2 * H, DK]), ALU.subtract).then_inc(s_oc.sem, 1)

            def scale(i, par):
                s_osq.wait(dve, i, 2)
                c_b.start(i, 4)
                c_b.link(nc.vector.reduce_sum(ro[:], osq[:].rearrange("p (h v) -> p h v", v=DK), axis=X))
                s_epsq.wait(dve, i, 1)
                c_b.link(nc.vector.scalar_tensor_tensor(out=osum[:], in0=ro[:], scalar=1.0 / DK, in1=epsq[par][:],
                                                        op0=ALU.mult, op1=ALU.add))
                inverse_sqrt(nc, c_b, ro[:], osum[:], tb[:], gb[:])
                c_b.end()
                nc.vector.tensor_tensor(oc[:].rearrange("p (h v) -> p h v", v=DK), oc[:].rearrange("p (h v) -> p h v", v=DK),
                                        ro[:][:, :, None].to_broadcast([P, B * H, DK]), ALU.mult).then_inc(s_onn.sem, 1)

            def gated(i, par):
                for h in range(2):
                    s_oga.wait(dve, i, h + 1)
                    nc.vector.tensor_tensor(og[:, h, :], og[:, h, :], gate[par][:, h, :], ALU.mult).then_inc(s_ogg.sem, 1)
            run_places(dve, [(15 + 2 * b, mask_update(b)) for b in range(B)]
                       + [(24, gated), (0, norm), (2, low), (11, values)]
                       + [(12 + t, mask_scores(t)) for t in range(8)]
                       + [(11, masks), (3, logit), (8, conv(5)), (9, sums((0, 1))), (10, sums((2, 3))), (10, key_norm),
                          (21, centre), (22, scale), (4, conv(0)), (5, conv(1)), (6, conv(2)), (7, conv(3)), (7, conv(4))])

        @block.scalar
        def _(act):
            def norm(i, par):
                s_rstd.wait(act, i, 1)
                xn_out.wait_before(act, i, 1, 16)
                s_xt.wait_before(act, i, 1, 2)
                for b in range(B):
                    act.activation(xn[:, b, :], xs[:, b, :], ACT.Identity, scale=rstd[:, b:b + 1],
                                   bias=nbias[:, b:b + 1]).then_inc(s_xn.sem, 1)

            def high(i, par):
                for h in range(2):
                    s_xt.wait(act, i, h + 1)
                    if h == 0:
                        s_proj.wait_before(act, i, 1, 8)
                    act.activation(xh[:, h, :], bank(f"x{h}")[:], ACT.Copy).then_inc(s_xh.sem, 1)

            def evac(blk):
                def f(i, par):
                    s_proj.wait(act, i, blk + 1)
                    if blk == 0:
                        s_hist.wait_before(act, i, 1, 1)
                    act.activation(pre[:, blk, :, 3:], bank(f"p{blk}")[:].rearrange("p (b t) -> p b t", b=B), ACT.Copy,
                                   scale=UNSCALE).then_inc(s_p.sem, 1)
                return f

            def evac_gate(i, par):
                for h in range(2):
                    s_proj.wait(act, i, 7 + h)
                    if h == 0:
                        s_ogg.wait_before(act, i, 2, 2)
                    act.activation(gate[par][:, h, :], bank(f"g{h}")[:], ACT.Copy, scale=UNSCALE).then_inc(s_g.sem, 1)

            def silu(blk):
                def f(i, par):
                    s_conv.wait(act, i, blk + 1)
                    if blk == 0:
                        s_o.wait_before(act, i, 2, 8)
                        s_ql.wait_before(act, i, 2, 2)
                    if blk == 2:
                        s_qkt.wait_before(act, i, 1, 4)
                        s_kl.wait_before(act, i, 1, 2)
                    if blk == 4:
                        s_vtt.wait_before(act, i, 1, 2)
                    act.activation((qt[par], kt, vt)[blk // 2][:, blk % 2, :], acc[:, blk % 2, :], ACT.Silu).then_inc(s_silu.sem, 1)
                return f

            def query_high(i, par):
                for h in range(2):
                    s_silu.wait(act, i, h + 1)
                    if h == 0:
                        s_s.wait_before(act, i, 2, 8)
                    act.activation(qh[par][:, h, :], qt[par][:, h, :], ACT.Copy).then_inc(s_qh.sem, 1)

            def key_high(i, par):
                for h in range(2):
                    s_silu.wait(act, i, h + 3)
                    if h == 0:
                        s_km.wait_before(act, i, 1, 8)
                    act.activation(khf[:, h, :], kt[:, h, :], ACT.Copy).then_inc(s_kh.sem, 1)

            def squares(bs):
                def f(i, par):
                    for b in bs:
                        s_qkt.wait(act, i, b + 1)
                        if b == 0:
                            s_u.wait_before(act, i, 2, 4)
                        if b < 2:
                            s_ssq.wait_before(act, i, 1, 3 + b)
                            s_vp.wait_before(act, i, 1, 2)
                        else:
                            s_ssq.wait(act, i, b - 1)
                        act.activation(kn[par][:, b, :], bank(f"qk{b}")[:, 256:512], ACT.Copy).then_inc(s_kn.sem, 1)
                        act.activation(sq[:, b % 2, :], bank(f"qk{b}")[:], ACT.Square).then_inc(s_sq.sem, 1)
                return f

            def spread(i, par):
                s_vp.wait(act, i, 2)
                s_o.wait_before(act, i, 2, 8)
                for s in range(2):
                    for e in range(2):
                        src = vp[par][64 * s:64 * s + 64, :, :].rearrange("p b (k e v) -> p (b k) e v", e=2, v=DK)[:, :, e, :]
                        dst = vbd[par][64 * e:64 * e + 64, :, s, :, 16 * e:16 * e + 16]
                        act.activation(dst, src.rearrange("p (b k) v -> p b k v", b=B), ACT.Copy).then_inc(s_vbd.sem, 1)

            def out(b):
                def f(i, par):
                    s_u.wait(act, i, b + 1)
                    if b == 0:
                        s_on.wait_before(act, i, 1, 2)
                    act.activation(ot[:, :, b * P:(b + 1) * P], oubank[:, 0:256].rearrange("p (h t) -> p h t", h=2),
                                   ACT.Copy).then_inc(s_oe.sem, 1)
                return f

            def square(i, par):
                for n in range(2):
                    s_oc.wait(act, i, n + 1)
                    act.activation(osq[:, n * W:(n + 1) * W], oc[:, n * W:(n + 1) * W], ACT.Square).then_inc(s_osq.sem, 1)

            def affine(i, par):
                s_ogl.wait_before(act, i, 1, 2)
                for h in range(2):
                    s_ont.wait(act, i, h + 1)
                    act.activation(og[:, h, :], bank(f"ont{h}")[:], ACT.Identity, scale=gam[:], bias=bet[:]).then_inc(s_oga.sem, 1)

            def out_high(i, par):
                for h in range(2):
                    s_ogg.wait(act, i, h + 1)
                    if h == 0:
                        s_wo.wait_before(act, i, 1, 2)
                    act.activation(ogh[:, h, :], og[:, h, :], ACT.Copy).then_inc(s_ogh.sem, 1)

            def evac_out(i, par):
                at_out.wait_before(act, i, 1, 16)
                for n in range(2):
                    s_wo.wait(act, i, n + 1)
                    act.activation(at[:, 2 * n:2 * n + 2, :], bank(f"wo{n}")[:].rearrange("p (b c) -> p b c", b=2), ACT.Copy,
                                   scale=UNSCALE).then_inc(s_at.sem, 1)
            run_places(act, [(15 + 2 * b, out(b)) for b in range(B)]
                       + [(8, silu(3)), (8, silu(4)), (8, evac_gate), (24, out_high), (8, squares((0, 1))), (8, key_high),
                          (1, norm), (9, silu(5)), (9, squares((2, 3))),
                          (2, high), (11, spread),
                          (4, evac(0)), (28, evac_out),
                          (5, evac(1)), (5, evac(2)), (5, silu(0)), (21, square),
                          (6, silu(1)), (6, evac(3)),
                          (7, evac(4)), (7, evac(5)), (7, silu(2)), (23, affine), (7, query_high)])

        @block.gpsimd
        def _(pool):
            def tap(blk):
                def f(i, par):
                    s_p.wait(pool, i, blk + 1)
                    if blk < 2:
                        s_silu.wait_before(pool, i, 1, 5 + blk)
                    else:
                        s_silu.wait(pool, i, blk - 1)
                    apart(pool, passed)
                    pool.tensor_scalar(acc[:, blk % 2, :].rearrange("p (b t) -> p b t", b=B), pre[:, blk, :, 3:],
                                       taps[:, blk, 3:4], None, ALU.mult).then_inc(s_tap.sem, 1)
                return f

            def query_low(i, par):
                for h in range(2):
                    s_qh.wait(pool, i, h + 1)
                    if h == 0:
                        s_s.wait_before(pool, i, 2, 8)
                    pool.tensor_tensor(ql[par][:, h, :], qt[par][:, h, :], qh[par][:, h, :], ALU.subtract).then_inc(s_ql.sem, 1)

            def key_low(i, par):
                for h in range(2):
                    s_kh.wait(pool, i, h + 1)
                    if h == 0:
                        s_km.wait_before(pool, i, 1, 8)
                    pool.tensor_tensor(klf[:, h, :], kt[:, h, :], khf[:, h, :], ALU.subtract).then_inc(s_kl.sem, 1)

            def add(b):
                def f(i, par):
                    s_um.wait(pool, i, b + 1)
                    s_st.wait_before(pool, i, 1, b + 1)
                    pool.tensor_tensor(state[:, b, :, :], state[:, b, :, :], um[b % 2][:], ALU.add).then_inc(s_st.sem, 1)
                return f

            def out_low(i, par):
                for h in range(2):
                    s_ogh.wait(pool, i, h + 1)
                    if h == 0:
                        s_wo.wait_before(pool, i, 1, 2)
                    pool.tensor_tensor(ogl[:, h, :], og[:, h, :], ogh[:, h, :], ALU.subtract).then_inc(s_ogl.sem, 1)
            run_places(pool, [(15 + 2 * b, add(b)) for b in range(B)]
                       + [(4, tap(0)), (5, tap(1)), (6, tap(2)), (7, tap(3)), (7, tap(4)), (8, tap(5)), (8, query_low),
                          (9, key_low), (25, out_low)])

        @block.tensor
        def _(pe):
            mm = nc.tensor.matmul

            def flip(i, par):
                s_xn.wait(pe, i, 4)
                for h in range(2):
                    wait_bank(pe, f"x{h}", i)
                    for b in range(B):
                        last = nc.tensor.transpose(bank(f"x{h}")[:, b * P:(b + 1) * P], xn[:, b, h * P:(h + 1) * P], ident[:])
                    last.then_inc(s_xt.sem, 1)

            def route(i, par):
                s_xl.wait(pe, i, 2)
                wait_bank(pe, "route", i)
                for b in range(B):
                    n = 0
                    for lhs, rhs in ((xh, rh), (xh, rl), (xl, rh)):
                        for h in range(2):
                            last = mm(bank("route")[:, b * E:(b + 1) * E], lhs[:, h, b * P:(b + 1) * P], rhs[:, h, :],
                                      start=n == 0, stop=n == 5)
                            n += 1
                last.then_inc(s_lg.sem, 1)

            def project(blk):
                name = f"p{blk}" if blk < 6 else f"g{blk - 6}"

                def f(i, par):
                    m, o = divmod(blk, 2)
                    if blk == 0:
                        s_xl.wait(pe, i, 2)
                    wait_bank(pe, name, i)
                    n = 0
                    for lhs, rhs in ((wh, xh), (wl, xh), (wh, xl)):
                        for h in range(2):
                            last = mm(bank(name)[:], lhs[:, m, h, o * P:(o + 1) * P], rhs[:, h, :],
                                      start=n == 0, stop=n == 5)
                            n += 1
                    last.then_inc(s_proj.sem, 1)
                return f

            def flip_qk(b):
                def f(i, par):
                    if b == 0:
                        s_silu.wait(pe, i, 4)
                    wait_bank(pe, f"qk{b}", i)
                    for n, src in enumerate((qt[par], kt)):
                        for h in range(2):
                            last = nc.tensor.transpose(bank(f"qk{b}")[:, n * 256 + h * P:n * 256 + (h + 1) * P],
                                                       src[:, h, b * P:(b + 1) * P], ident[:])
                    last.then_inc(s_qkt.sem, 1)
                return f

            def flip_v(i, par):
                s_silu.wait(pe, i, 6)
                for n in range(2):
                    wait_bank(pe, f"v{n}t", i)
                    for b in range(2):
                        for h in range(2):
                            last = nc.tensor.transpose(bank(f"v{n}t")[:, b * 256 + h * P:b * 256 + (h + 1) * P],
                                                       vt[:, h, (2 * n + b) * P:(2 * n + b + 1) * P], ident[:])
                    last.then_inc(s_vtt.sem, 1)

            def scores(t):
                def f(i, par):
                    b, h = divmod(t, 2)
                    if t == 0:
                        s_km.wait(pe, i, 8)
                        s_ql.wait(pe, i, 2)
                        s_qh.wait(pe, i, 2)
                        s_sc.wait_before(pe, i, 1, 8)
                    else:
                        s_sc.wait(pe, i, t)
                    for r in range(4):
                        rows = slice(32 * r, 32 * r + 32)
                        n = 0
                        for km, q in ((kmh, qh), (kmh, ql), (kml, qh)):
                            mm(sbank[:, r, 0:P], km[par][rows, h, 2 * b, :, :].rearrange("p e s -> p (e s)"),
                               q[par][rows, h, b * P:(b + 1) * P], start=n == 0, stop=n == 2)
                            n += 1
                        n = 0
                        for km, q in ((kmh, qh), (kmh, ql), (kml, qh)):
                            last = mm(sbank[:, r, P:192], km[par][rows, h, 2 * b + 1, :, :].rearrange("p e s -> p (e s)"),
                                      q[par][rows, h, b * P + 64:(b + 1) * P], start=n == 0, stop=n == 2)
                            n += 1
                    last.then_inc(s_s.sem, 1)
                return f

            def outputs(t):
                def f(i, par):
                    b, h = divmod(t, 2)
                    if h == 0:
                        s_st.wait_before(pe, i, 1, b + 1)
                        if b == 0:
                            s_um.wait_before(pe, i, 1, B)
                        else:
                            s_um.wait(pe, i, b)
                    if t == 0:
                        s_vbd.wait(pe, i, 4)
                        s_kn.wait(pe, i, 4)
                    s_sc.wait(pe, i, t + 1)
                    o = oubank
                    mm(o[:, h * P:(h + 1) * P], state[:, b, h, :], qt[par][:, h, b * P:(b + 1) * P],
                       start=True, stop=False, skip_group_check=True)
                    for r in range(4):
                        rows = slice(32 * r, 32 * r + 32)
                        mm(o[rows, h * P:(h + 1) * P], vbd[par][:, b, 0, 4 * h + r, :], sc[t % 2][:, r, 0:P],
                           start=False, stop=False, skip_group_check=True)
                        last = mm(o[rows, h * P + 64:(h + 1) * P], vbd[par][:, b, 1, 4 * h + r, :], sc[t % 2][:, r, P:192],
                                  start=False, stop=True, skip_group_check=True)
                    last.then_inc(s_o.sem, 1)
                    if h == 1:
                        for g in range(2):
                            last = mm(o[:, 256 + g * P:256 + (g + 1) * P], kn[par][:, b, g * P:(g + 1) * P],
                                      vp[par][:, b, g * P:(g + 1) * P], start=True, stop=True)
                        last.then_inc(s_u.sem, 1)
                return f

            def out_rows(n):
                def f(i, par):
                    s_oe.wait(pe, i, 2 * n + 2)
                    wait_bank(pe, f"on{n}", i)
                    for b in range(2):
                        for h in range(2):
                            last = nc.tensor.transpose(bank(f"on{n}")[:, b * 256 + h * P:b * 256 + (h + 1) * P],
                                                       ot[:, h, (2 * n + b) * P:(2 * n + b + 1) * P], ident[:])
                    last.then_inc(s_on.sem, 1)
                return f

            def out_columns(i, par):
                s_onn.wait(pe, i, 1)
                for h in range(2):
                    wait_bank(pe, f"ont{h}", i)
                    for b in range(B):
                        last = nc.tensor.transpose(bank(f"ont{h}")[:, b * P:(b + 1) * P],
                                                   oc[:, b * D + h * P:b * D + (h + 1) * P], ident[:])
                    last.then_inc(s_ont.sem, 1)

            def project_out(i, par):
                s_ogh.wait(pe, i, 2)
                s_ogl.wait(pe, i, 2)
                for m in range(2):
                    wait_bank(pe, f"wo{m}", i)
                    for b in range(2):
                        n = 0
                        for lhs, rhs in ((ogh, wh), (ogh, wl), (ogl, wh)):
                            for h in range(2):
                                last = mm(bank(f"wo{m}")[:, b * 256:(b + 1) * 256], lhs[:, h, (2 * m + b) * P:(2 * m + b + 1) * P],
                                          rhs[:, 4, h, :], start=n == 0, stop=n == 5)
                                n += 1
                    last.then_inc(s_wo.sem, 1)
            pieces = []
            for t in range(8):
                pieces.append((12 + t, scores(t)))
            for t in range(8):
                pieces.append((13 + t, outputs(t)))
            run_places(pe, pieces + [(8, project(6)), (8, project(7)), (8, flip_qk(0)), (8, flip_qk(1)),
                                     (9, flip_qk(2)), (9, flip_qk(3)), (1, flip), (10, flip_v), (3, route), (3, project(0)),
                                     (27, project_out), (4, project(1)), (4, project(2)), (20, out_rows(0)), (21, out_rows(1)),
                                     (5, project(3)), (6, project(4)), (6, project(5)), (23, out_columns)])


def routing(nc, a, sb_, sem_, ident, logits, wts, slots, ids, eid, w1h, w1l, w2h, w2l, brow, ones3):
    ctx = ExitStack()
    with ctx:
        def sb(name, shape, dt=F32):
            return sb_(name, shape, dt, ctx)

        def sem(name):
            return sem_(name, ctx)

        prob = sb("prob", [P, NT, E])
        work = sb("work", [P, NT, E])
        pick = [sb(f"pick{n}", [P, NT, E]) for n in range(2)]
        scan = [sb(f"scan{n}", [P, NT, E]) for n in range(2)]
        top = sb("top", [P, 2, NT])
        col = sb("col", [P, NT])
        both = sb("both", [P, NT, E], F16)
        tri32 = sb("tri32", [P, P])
        tri = sb("tri", [P, P], F16)
        ones = sb("ones", [P, P], F16)
        desc = sb("desc", [P, E])
        ends = sb("ends", [P, E])
        nti = sb("nti", [P, E], I32)
        ntf = sb("ntf", [P, E])
        base = sb("base", [P, E])
        one16 = sb("one16", [P, E])
        jt = sb("jt", [P, SLOT_TILES])
        jti = sb("jti", [P, SLOT_TILES], I32)
        cmpj = sb("cmpj", [P, SLOT_TILES, E])
        low = sb("low", [P, 2 * NT], I32)
        where = sb("where", [P, 2, NT], I32)
        tok = sb("tok", [P, NT], I32)
        zero = sb("zero", [P, SLOT_TILES], I32)
        wcol = sb("wcol", [P, 2, 8], I32)
        tcol = sb("tcol", [P, 8], I32)
        stage = [sb(f"stage{n}", [P, 4 * D]) for n in range(2)]
        bf = sb("bf", [E, 2 * D])
        bparts = [sb(f"bpart{n}", [E, 2 * D], F16) for n in range(3)]
        bank = ctx.enter_context(nc.psum_tensor("rank_bank", [P, 4, 512], F32))

        r_const, r_iota, r_exp, r_max, r_mask, r_rank, r_slot = (sem(s) for s in (
            "r_const", "r_iota", "r_exp", "r_max", "r_mask", "r_rank", "r_slot"))
        zeroed, scattered, id_in, copied = (sem(s) for s in ("zeroed", "scattered", "id_in", "copied"))
        w_in = [sem(f"w_in{n}") for n in range(2)]
        w_hi, w_lo, b_in, b_ok, b_out = (sem(s) for s in ("w_hi", "w_lo", "b_in", "b_ok", "b_out"))
        ch, passed = sem("chain_r"), sem("passed_r")
        NC = 2 * E // 2

        def chunk(m):
            src = a["w1"] if m < NC // 2 else a["w2"]
            hi, lo = (w1h, w1l) if m < NC // 2 else (w2h, w2l)
            k = m % (NC // 2)
            return src[:, 2 * k:2 * k + 2], [t[:, 2 * k:2 * k + 2].rearrange("p e h n -> p (e h n)") for t in (hi, lo)]

        with nc.Block() as block:
            @block.sync
            def _(sp):
                sp.dma_start(tri32[:], a["tri"]).then_inc(r_const, 16)
                sp.dma_start(desc[:], a["desc"]).then_inc(r_const, 16)
                sp.dma_start(bf[:].rearrange("e (k n) -> e k n", k=2), a["b12"]).then_inc(b_in, 16)
                for m in range(NC):
                    if m >= 2:
                        sp.wait_ge(w_lo, m - 1)
                    sp.dma_start(stage[m % 2][:].rearrange("p (e h n) -> p e h n", e=2, h=2), chunk(m)[0]).then_inc(w_in[m % 2], 16)
                sp.wait_ge(b_ok, 5)
                for n in range(3):
                    for k in range(2):
                        sp.dma_start(brow[n:n + 1, k, :, :], bparts[n][:, k * D:(k + 1) * D]).then_inc(b_out, 16)
                sp.wait_ge(b_out, 6 * 16)
                sp.wait_ge(r_iota, 5)
                sp.dma_start(a["slot_ids"].rearrange("(p j) o -> p (j o)", p=P), zero[:]).then_inc(zeroed, 16)
                sp.wait_ge(scattered, 16 * 2 * NT)
                sp.dma_start(ids[:], a["slot_ids"].rearrange("(p j) o -> p (j o)", p=P)).then_inc(id_in, 16)
                sp.wait_ge(id_in, 16)

            @block.scalar
            def _(act):
                act.wait_ge(r_max, 1)
                act.activation(work[:], work[:], ACT.Exp).then_inc(r_exp, 1)
                for m in range(NC):
                    act.wait_ge(w_in[m % 2], 16 * (m // 2 + 1))
                    act.activation(chunk(m)[1][0], stage[m % 2][:], ACT.Copy, scale=SCALE_W).then_inc(w_hi, 1)

            @block.vector
            def _(dve):
                c = Chain(dve, ch, 0)
                link, v = c.link, nc.vector

                def wide(t):
                    return t[:, :, None].to_broadcast([P, NT, E])

                def per_expert(t):
                    return t[:, None, :].to_broadcast([P, NT, E])
                link(v.reduce_max(col[:], logits[:], axis=X))
                v.tensor_tensor(work[:], logits[:], wide(col), ALU.subtract).then_inc(r_max, 1)
                dve.wait_ge(r_exp, 1)
                link(v.reduce_sum(col[:], work[:], axis=X))
                link(v.reciprocal(col[:], col[:]))
                link(v.tensor_tensor(prob[:], work[:], wide(col), ALU.mult))
                dve.wait_ge(r_const, 32)
                for s in range(2):
                    link(v.reduce_max(top[:, s, :], prob[:], axis=X))
                    link(v.tensor_tensor(work[:], prob[:], wide(top[:, s, :]), ALU.is_equal))
                    link(v.tensor_tensor(work[:], work[:], per_expert(desc), ALU.mult))
                    link(v.reduce_max(col[:], work[:], axis=X))
                    link(v.tensor_tensor(pick[s][:], per_expert(desc), wide(col), ALU.is_equal))
                    if s == 0:
                        link(v.scalar_tensor_tensor(out=prob[:], in0=pick[0][:], scalar=-2.0, in1=prob[:], op0=ALU.mult, op1=ALU.add))
                link(v.tensor_tensor(col[:], top[:, 0, :], top[:, 1, :], ALU.add))
                link(v.tensor_scalar(col[:], col[:], 1e-9, None, ALU.max))
                link(v.reciprocal(col[:], col[:]))
                link(v.tensor_tensor(wts[:], top[:], col[:, None, :].to_broadcast([P, 2, NT]), ALU.mult))
                link(v.tensor_tensor(both[:], pick[0][:], pick[1][:], ALU.add))
                link(v.memset(ones[:], 1.0))
                link(v.memset(ones3[:], 1.0))
                link(v.memset(one16[:], 1.0))
                v.tensor_copy(tri[:], tri32[:]).then_inc(r_mask, 1)
                dve.wait_ge(b_in, 16)
                link(v.tensor_scalar(bf[:], bf[:], SCALE_W, None, ALU.mult))
                for n in range(3):
                    v.tensor_copy(bparts[n][:], bf[:]).then_inc(b_ok, 1)
                    dve.wait_ge(b_ok, 2 * n + 1)
                    if n < 2:
                        v.tensor_tensor(bf[:], bf[:], bparts[n][:], ALU.subtract).then_inc(b_ok, 1)
                        dve.wait_ge(b_ok, 2 * n + 2)
                dve.wait_ge(r_rank, 1)
                link(v.tensor_copy(scan[0][:].rearrange("p t e -> p (t e)"), bank[:, 2:4, :].rearrange("p k n -> p (k n)")))
                link(v.tensor_copy(work[:], scan[0][:]))
                s, d = 0, 1
                while d < NT:
                    link(v.tensor_tensor(scan[1 - s][:, d:, :], scan[s][:, d:, :], scan[s][:, :NT - d, :], ALU.add))
                    link(v.tensor_copy(scan[1 - s][:, :d, :], scan[s][:, :d, :]))
                    s, d = 1 - s, 2 * d
                total = scan[s][:, NT - 1, :]
                link(v.tensor_scalar(nti[:], total, float(P - 1), None, ALU.add))
                link(v.tensor_scalar(nti[:], nti[:], 7, None, ALU.arith_shift_right))
                link(v.tensor_copy(ntf[:], nti[:]))
                link(v.tensor_tensor_scan(out=ends[:], data0=one16[:], data1=ntf[:], initial=0.0, op0=ALU.mult, op1=ALU.add))
                link(v.tensor_tensor(base[:], ends[:], ntf[:], ALU.subtract))
                link(v.tensor_scalar(base[:], base[:], float(P), None, ALU.mult))
                off = scan[1 - s]
                link(v.tensor_tensor(off[:], scan[s][:], work[:], ALU.subtract))
                link(v.tensor_tensor(off[:], off[:], per_expert(base), ALU.add))
                link(v.tensor_tensor(off[:].rearrange("p t e -> p (t e)"), off[:].rearrange("p t e -> p (t e)"),
                                     bank[:, 0:2, :].rearrange("p k n -> p (k n)"), ALU.add))
                for s in range(2):
                    link(v.tensor_tensor(work[:], pick[s][:], off[:], ALU.mult))
                    link(v.reduce_sum(col[:], work[:], axis=X))
                    link(v.tensor_copy(slots[:, s, :], col[:]))
                sl = slots[:].rearrange("p s t -> p (s t)")
                wh_ = where[:].rearrange("p s t -> p (s t)")
                link(v.tensor_scalar(low[:], sl, P - 1, None, ALU.bitwise_and))
                link(v.tensor_scalar(wh_, sl, 7, None, ALU.arith_shift_right))
                v.scalar_tensor_tensor(out=wh_, in0=low[:], scalar=float(SLOT_TILES), in1=wh_,
                                       op0=ALU.mult, op1=ALU.add).then_inc(r_slot, 1)
                dve.wait_ge(r_iota, 5)
                link(v.tensor_copy(jt[:], jti[:]))
                link(v.tensor_tensor(cmpj[:], ends[:, None, :].to_broadcast([P, SLOT_TILES, E]),
                                     jt[:, :, None].to_broadcast([P, SLOT_TILES, E]), ALU.is_le))
                link(v.reduce_sum(jt[:], cmpj[:], axis=X))
                link(v.tensor_scalar(eid[:], jt[:], float(E - 1), None, ALU.min))
                for m in range(NC):
                    dve.wait_ge(w_hi, m + 1)
                    hi, lo = chunk(m)[1]
                    v.scalar_tensor_tensor(out=lo, in0=stage[m % 2][:], scalar=SCALE_W, in1=hi,
                                           op0=ALU.mult, op1=ALU.subtract).then_inc(w_lo, 1)

            @block.tensor
            def _(pe):
                pe.wait_ge(r_mask, 1)
                for n, lhs in enumerate((tri, ones)):
                    for k in range(2):
                        last = nc.tensor.matmul(bank[:, 2 * n + k, :], lhs[:], both[:, 32 * k:32 * k + 32, :].rearrange("p t e -> p (t e)"),
                                                start=True, stop=True)
                last.then_inc(r_rank, 1)

            @block.gpsimd
            def _(pool):
                pool.iota(tok[:], [[P, NCH], [L, B]], base=0, channel_multiplier=1).then_inc(r_iota, 1)
                pool.iota(jti[:], [[1, SLOT_TILES]], base=0, channel_multiplier=0).then_inc(r_iota, 1)
                pool.memset(zero[:], 0).then_inc(r_iota, 1)
                pool.memset(wcol[:], 0).then_inc(r_iota, 1)
                pool.memset(tcol[:], 0).then_inc(r_iota, 1)
                pool.wait_ge(r_iota, 5)
                pool.wait_ge(zeroed, 16)
                pool.wait_ge(r_slot, 1)
                with pool.Fori(0, NT // 8, 1) as g:
                    pool.tensor_copy(wcol[:], where[:, :, bass.ds(g * 8, 8)]).then_inc(copied, 1)
                    pool.tensor_copy(tcol[:], tok[:, bass.ds(g * 8, 8)]).then_inc(copied, 1)
                    pool.wait_ge(copied, g * 2 + 2)
                    apart(pool, passed)
                    for k in range(8):
                        for s in range(2):
                            pool.indirect_dma_start(out=a["slot_ids"], out_offset=bass.IndirectOffsetOnAxis(ap=wcol[:, s, k:k + 1], axis=0),
                                                    in_=tcol[:, k:k + 1], in_offset=None).then_inc(scattered, 16)
                    pool.wait_ge(scattered, g * 256 + 256)


def experts(nc, a, sb_, sem_, ident, ids, eid, w1h, w1l, w2h, w2l, brow, ones3):
    ctx = ExitStack()
    with ctx:
        def sb(name, shape, dt=F32):
            return sb_(name, shape, dt, ctx)

        def sem(name):
            return sem_(name, ctx)

        NU = SLOT_TILES // 2
        ic = [sb(f"ic{n}", [P, 2], I32) for n in range(2)]
        xg = [sb(f"xg{n}", [P, 2, D]) for n in range(2)]
        xth = [sb(f"xth{n}", [P, 2, 2, P], F16) for n in range(2)]
        xtl = [sb(f"xtl{n}", [P, 2, 2, P], F16) for n in range(2)]
        st = [sb(f"st{n}", [P, 2, 6]) for n in range(2)]
        mv = [sb(f"mv{n}", [P, 2, 2]) for n in range(2)]
        vr = [sb(f"vr{n}", [P, 2]) for n in range(2)]
        tt = [sb(f"tt{n}", [P, 2]) for n in range(2)]
        gi = [sb(f"gi{n}", [P, 2], I32) for n in range(2)]
        rs = [sb(f"rs{n}", [P, 2]) for n in range(2)]
        nb = [sb(f"nb{n}", [P, 2]) for n in range(2)]
        hn = [sb(f"hn{n}", [P, 2, HID]) for n in range(2)]
        gl = [sb(f"gl{n}", [P, 2, 2, P]) for n in range(2)]
        glh = [sb(f"glh{n}", [P, 2, 2, P], F16) for n in range(2)]
        gll = [sb(f"gll{n}", [P, 2, 2, P], F16) for n in range(2)]
        ys = [sb(f"ys{n}", [P, 2, D]) for n in range(2)]
        g1 = sb("g1", [P, 2, E])
        be1 = sb("be1", [P, 2, E])

        def banks(name):
            return [ctx.enter_context(nc.psum_tensor(f"{name}{n}", [P, 512], F32)) for n in range(2)]
        xb, hb, tb, yb = banks("xb"), banks("hb"), banks("tb"), banks("yb")

        def sig(name, per):
            return Signal(sem(name), per)
        const = sem("f_const")
        f_ic, f_xt, f_xh, f_xl, f_h = sig("f_ic", 1), sig("f_xt", 1), sig("f_xh", 1), sig("f_xl", 1), sig("f_h", 1)
        f_in = [sem(f"f_in{n}") for n in range(2)]
        f_out = [sem(f"f_out{n}") for n in range(2)]
        f_rs, f_hn, f_ht, f_gl, f_glh, f_gll, f_y, f_ys = (
            sig("f_rs", 1), sig("f_hn", 2), sig("f_ht", 1), sig("f_gl", 4), sig("f_glh", 1), sig("f_gll", 1),
            sig("f_y", 1), sig("f_ys", 1))
        ch, passed = sem("chain_f"), sem("passed_f")

        def run(eng, stages):
            last_lag = max(lag for lag, _ in stages)

            def step(s, par, static):
                for lag, f in stages:
                    if static and not 0 <= s - lag < NU:
                        continue
                    f(s - lag, (par - lag) % 2)
            first = last_lag + last_lag % 2 + 2
            for s in range(first):
                step(s, s % 2, True)
            with eng.Fori(first // 2, NU // 2) as k:
                step(k * 2, 0, False)
                step(k * 2 + 1, 1, False)
            for s in range(NU, NU + last_lag):
                step(s, s % 2, True)

        with nc.Block() as block:
            @block.sync
            def _(sp):
                sp.dma_start(g1[:], a["g1"]).then_inc(const, 16)
                sp.dma_start(be1[:], a["be1"]).then_inc(const, 16)

                def store(u, par):
                    f_ys.wait(sp, u, 1)
                    apart(sp, passed)
                    sp.dma_start(a["y_rows"][bass.ds(u * 256, 256), :].rearrange("(k p) c -> p k c", p=P), ys[par][:]).then_inc(f_out[par], 16)
                run(sp, [(5, store)])
                for n in range(2):
                    sp.wait_ge(f_out[n], NU // 2 * 16)

            @block.gpsimd
            def _(pool):
                def gather(u, par):
                    f_xt.wait_before(pool, u, 2, 1)
                    pool.tensor_copy(ic[par][:], ids[:, bass.ds(u * 2, 2)]).then_inc(f_ic.sem, 1)
                    f_ic.wait(pool, u, 1)
                    apart(pool, passed)
                    for k in range(2):
                        pool.indirect_dma_start(out=xg[par][:, k, :], out_offset=None, in_=a["xn_rows"].rearrange("b l c -> (b l) c"),
                                                in_offset=bass.IndirectOffsetOnAxis(ap=ic[par][:, k:k + 1], axis=0)).then_inc(f_in[par], 16)

                def gelu_low(u, par):
                    f_glh.wait(pool, u, 1)
                    f_y.wait_before(pool, u, 2, 1)
                    pool.tensor_tensor(gll[par][:], gl[par][:], glh[par][:], ALU.subtract).then_inc(f_gll.sem, 1)
                run(pool, [(0, gather), (4, gelu_low)])

            @block.tensor
            def _(pe):
                mm = nc.tensor.matmul

                def flip(u, par):
                    pe.wait_ge(f_in[par], after(u, par, 32))
                    f_xl.wait_before(pe, u, 2, 1)
                    for k in range(2):
                        for h in range(2):
                            last = nc.tensor.transpose(xb[par][:, (2 * k + h) * P:(2 * k + h + 1) * P], xg[par][:, k, h * P:(h + 1) * P], ident[:])
                    last.then_inc(f_xt.sem, 1)

                def product(u, par, out, hi, lo, wh, wl, which):
                    for k in range(2):
                        e = pe.value_load(eid[0:1, bass.ds(u * 2 + k, 1)], min_val=0, max_val=E - 1)
                        o = out[par][:, k * 256:(k + 1) * 256]
                        for h in range(2):
                            mm(o, hi[par][:, k, h, :], wh[:, bass.ds(e, 1), h, :].rearrange("p e n -> p (e n)"), start=h == 0, stop=False)
                            mm(o, hi[par][:, k, h, :], wl[:, bass.ds(e, 1), h, :].rearrange("p e n -> p (e n)"), start=False, stop=False)
                            mm(o, lo[par][:, k, h, :], wh[:, bass.ds(e, 1), h, :].rearrange("p e n -> p (e n)"), start=False, stop=False)
                        last = mm(o, ones3[:], brow[0:3, which, bass.ds(e, 1), :].rearrange("p e n -> p (e n)"), start=False, stop=True)
                    return last

                def first(u, par):
                    f_xl.wait(pe, u, 1)
                    f_hn.wait_before(pe, u, 2, 2)
                    product(u, par, hb, xth, xtl, w1h, w1l, 0).then_inc(f_h.sem, 1)

                def flip_back(u, par):
                    f_hn.wait(pe, u, 2)
                    f_gl.wait_before(pe, u, 2, 4)
                    for k in range(2):
                        for h in range(2):
                            last = nc.tensor.transpose(tb[par][:, (2 * k + h) * P:(2 * k + h + 1) * P], hn[par][:, k, h * P:(h + 1) * P], ident[:])
                    last.then_inc(f_ht.sem, 1)

                def second(u, par):
                    f_glh.wait(pe, u, 1)
                    f_gll.wait(pe, u, 1)
                    f_ys.wait_before(pe, u, 2, 1)
                    product(u, par, yb, glh, gll, w2h, w2l, 1).then_inc(f_y.sem, 1)
                run(pe, [(5, second), (0, flip), (3, flip_back), (1, first)])

            @block.scalar
            def _(act):
                act.wait_ge(const, 32)

                def high(u, par):
                    f_xt.wait(act, u, 1)
                    f_h.wait_before(act, u, 2, 1)
                    act.activation(xth[par][:].rearrange("p k h s -> p (k h s)"), xb[par][:], ACT.Copy).then_inc(f_xh.sem, 1)

                def norm(u, par):
                    f_rs.wait(act, u, 1)
                    f_ht.wait_before(act, u, 2, 1)
                    for k in range(2):
                        act.activation(hn[par][:, k, :], hb[par][:, k * 256:(k + 1) * 256], ACT.Identity, scale=rs[par][:, k:k + 1],
                                       bias=nb[par][:, k:k + 1]).then_inc(f_hn.sem, 1)

                def gelu(u, par):
                    f_ht.wait(act, u, 1)
                    f_gll.wait_before(act, u, 2, 1)
                    for k in range(2):
                        e = act.value_load(eid[0:1, bass.ds(u * 2 + k, 1)], min_val=0, max_val=E - 1)
                        for h in range(2):
                            act.activation(gl[par][:, k, h, :], tb[par][:, (2 * k + h) * P:(2 * k + h + 1) * P], ACT.Gelu,
                                           scale=g1[:, h, bass.ds(e, 1)], bias=be1[:, h, bass.ds(e, 1)]).then_inc(f_gl.sem, 1)

                def out(u, par):
                    f_y.wait(act, u, 1)
                    act.wait_ge(f_out[par], after(u, par, 16) - 16)
                    act.activation(ys[par][:].rearrange("p k c -> p (k c)"), yb[par][:], ACT.Copy, scale=UNSCALE).then_inc(f_ys.sem, 1)

                def gelu_high(u, par):
                    f_gl.wait(act, u, 4)
                    f_y.wait_before(act, u, 2, 1)
                    act.activation(glh[par][:], gl[par][:], ACT.Copy).then_inc(f_glh.sem, 1)
                run(act, [(0, high), (2, norm), (3, gelu), (3, gelu_high), (5, out)])

            @block.vector
            def _(dve):
                c = Chain(dve, ch, LINKS_F, passed)

                def low(u, par):
                    f_xh.wait(dve, u, 1)
                    f_h.wait_before(dve, u, 2, 1)
                    nc.vector.tensor_tensor(xtl[par][:].rearrange("p k h s -> p (k h s)"), xb[par][:],
                                            xth[par][:].rearrange("p k h s -> p (k h s)"), ALU.subtract).then_inc(f_xl.sem, 1)

                def moments(u, par):
                    c.start(u)
                    f_h.wait(dve, u, 1)
                    f_hn.wait_before(dve, u, 2, 2)
                    for k in range(2):
                        c.count(nc.vector.bn_stats(st[par][:, k, :], hb[par][:, k * 256:(k + 1) * 256]))
                    c.wait(True)
                    for k in range(2):
                        c.count(nc.vector.bn_aggr(mv[par][:, k, :], st[par][:, k, :]))
                    c.wait()
                    c.link(nc.vector.tensor_scalar(vr[par][:], mv[par][:, :, 1], EPS * SCALE_W * SCALE_W, None, ALU.add))
                    inverse_sqrt(nc, c, rs[par][:], vr[par][:], tt[par][:], gi[par][:])
                    nc.vector.scalar_tensor_tensor(out=nb[par][:], in0=mv[par][:, :, 0], scalar=-1.0, in1=rs[par][:],
                                                   op0=ALU.mult, op1=ALU.mult).then_inc(f_rs.sem, 1)
                    c.end()

                run(dve, [(0, low), (1, moments)])


def combine(nc, a, sb_, sem_, wts, slots):
    ctx = ExitStack()
    with ctx:
        def sb(name, shape, dt=F32):
            return sb_(name, shape, dt, ctx)

        def sem(name):
            return sem_(name, ctx)
        xr = [sb(f"xr{n}", [P, B, D]) for n in range(2)]
        ar = [sb(f"ar{n}", [P, B, D]) for n in range(2)]
        yr = [sb(f"yr{n}", [P, 2, B, D]) for n in range(2)]
        sx = [sb(f"sx{n}", [P, 2, B], I32) for n in range(2)]
        wx = [sb(f"wx{n}", [P, 2, B]) for n in range(2)]
        passed = sem("passed_c")
        c_in = [sem(f"c_in{n}") for n in range(2)]
        c_y = [sem(f"c_y{n}") for n in range(2)]
        c_out = [sem(f"c_out{n}") for n in range(2)]

        def sig(name, per):
            return Signal(sem(name), per)
        c_idx, c_w, c_sum, c_one, c_two = sig("c_idx", 1), sig("c_w", 1), sig("c_sum", 1), sig("c_one", 4), sig("c_two", 4)

        def run(eng, f):
            for i in range(2):
                f(i, i)
            with eng.Fori(1, NCH // 2) as k:
                f(k * 2, 0)
                f(k * 2 + 1, 1)

        def rows(name, i):
            return a[name][:, bass.ds(i * P, P), :].rearrange("b t c -> t b c")

        with nc.Block() as block:
            @block.sync
            def _(sp):
                def load(i, par):
                    c_two.wait_before(sp, i, 2, 4)
                    apart(sp, passed)
                    sp.wait_ge(c_out[par], after(i, par, 16) - 16)
                    apart(sp, passed)
                    sp.dma_start(xr[par][:], rows("x", i)).then_inc(c_in[par], 16)
                    sp.dma_start(ar[par][:], rows("attn_rows", i)).then_inc(c_in[par], 16)
                run(sp, load)
                for n in range(2):
                    sp.wait_ge(c_out[n], NCH // 2 * 16)

            @block.scalar
            def _(act):
                def store(i, par):
                    c_two.wait(act, i, 4)
                    act.dma_start(rows("out", i), xr[par][:]).then_inc(c_out[par], 16)
                run(act, store)

            @block.gpsimd
            def _(pool):
                def gather(i, par):
                    c_two.wait_before(pool, i, 2, 4)
                    if isinstance(i, int) and i < 2:
                        pass
                    else:
                        pool.wait_ge(c_y[par], after(i, par, 128) - 128)
                    pool.tensor_copy(sx[par][:], slots[:, :, bass.ds(i * B, B)]).then_inc(c_idx.sem, 1)
                    c_idx.wait(pool, i, 1)
                    apart(pool, passed)
                    for s in range(2):
                        for b in range(B):
                            pool.indirect_dma_start(out=yr[par][:, s, b, :], out_offset=None, in_=a["y_rows"],
                                                    in_offset=bass.IndirectOffsetOnAxis(ap=sx[par][:, s, b:b + 1], axis=0)).then_inc(c_y[par], 16)
                run(pool, gather)

            @block.vector
            def _(dve):
                v = nc.vector

                def add(i, par):
                    dve.wait_ge(c_in[par], after(i, par, 32))
                    v.tensor_tensor(xr[par][:], xr[par][:], ar[par][:], ALU.add).then_inc(c_sum.sem, 1)
                    v.tensor_copy(wx[par][:], wts[:, :, bass.ds(i * B, B)]).then_inc(c_w.sem, 1)
                    c_sum.wait(dve, i, 1)
                    c_w.wait(dve, i, 1)
                    dve.wait_ge(c_y[par], after(i, par, 128))
                    for b in range(B):
                        v.scalar_tensor_tensor(out=xr[par][:, b, :], in0=yr[par][:, 0, b, :], scalar=wx[par][:, 0, b:b + 1],
                                               in1=xr[par][:, b, :], op0=ALU.mult, op1=ALU.add).then_inc(c_one.sem, 1)
                    for b in range(B):
                        c_one.wait(dve, i, b + 1)
                        v.scalar_tensor_tensor(out=xr[par][:, b, :], in0=yr[par][:, 1, b, :], scalar=wx[par][:, 1, b:b + 1],
                                               in1=xr[par][:, b, :], op0=ALU.mult, op1=ALU.add).then_inc(c_two.sem, 1)
                run(dve, add)

def layouts(i):
    import numpy as np
    f = lambda n: np.asarray(i[n])
    rows = lambda w: w.reshape(2, P, -1).transpose(1, 0, 2)
    p, s = np.arange(P)[:, None], np.arange(P)[None, :]
    key, t = np.arange(P)[:, None] % 64, np.arange(64)[None, :]
    causal = (t >= key).astype(np.float32)
    winit = np.zeros((P, B, 2, P), np.float32)
    for h in range(H):
        r = DK * (h % 8)
        winit[r:r + DK, :, h // 8, r:r + DK] = f("L0_attn_W_init")[0, h][:, None, :]
    a = {
        "x": f("L0_attn_hidden_states"),
        "wat": np.stack([rows(f(f"L0_attn_W{m}").T) for m in "qkvgo"]),
        "wr": rows(f("L0_ffn_Wr")),
        "br": np.broadcast_to(f("L0_ffn_br"), (P, E)),
        "taps": np.stack([f(f"L0_attn_conv_{m}").reshape(2, P, 4) for m in "qkv"]).reshape(6, P, 4).transpose(1, 0, 2),
        "gam": np.tile(f("L0_attn_ln_gamma"), P // DK)[:, None],
        "bet": np.tile(f("L0_attn_ln_beta"), P // DK)[:, None],
        "winit": winit,
        "ident": np.eye(P, dtype=np.float32),
        "cmask": np.concatenate([causal, np.ones((P, 64), np.float32), causal], 1),
        "bdmask": (p // DK == s // DK).astype(np.float32),
        "tri": (p < s).astype(np.float32),
        "desc": np.broadcast_to(E - np.arange(E, dtype=np.float32), (P, E)),
        "w1": f("L0_ffn_W1").reshape(E, 2, P, HID).transpose(2, 0, 1, 3),
        "w2": f("L0_ffn_W2").reshape(E, 2, P, D).transpose(2, 0, 1, 3),
        "b12": np.stack([f("L0_ffn_b1"), f("L0_ffn_b2")], 1),
        "g1": f("L0_ffn_g1").reshape(E, 2, P).transpose(2, 1, 0),
        "be1": f("L0_ffn_be1").reshape(E, 2, P).transpose(2, 1, 0),
        "parity": (p // DK % 2 == np.arange(2)[None, :]).astype(np.float32),
    }
    return {k: np.ascontiguousarray(v) for k, v in a.items()}


SCRATCH = {"xn_rows": ((B, L, D), F32), "attn_rows": ((B, L, D), F32), "y_rows": ((SLOT_TILES * P, D), F32),
           "slot_ids": ((SLOT_TILES * P, 1), I32)}


def kernel(**inputs):
    import numpy as np
    import concourse.bacc as bacc
    from concourse.bass_utils import run_bass_kernel_spmd

    nc = bacc.Bacc("TRN2", target_bir_lowering=False, num_devices=1)
    arrays = {f"in_{k}": v for k, v in layouts(inputs).items()}
    aps = {k[3:]: nc.dram_tensor(k, v.shape, mybir.dt.from_np(v.dtype), kind="ExternalInput").ap() for k, v in arrays.items()}
    for name, (shape, dtype) in SCRATCH.items():
        aps[name] = nc.dram_tensor(name, shape, dtype, kind="Internal").ap()
    aps["out"] = nc.dram_tensor("out", (B, L, D), F32, kind="ExternalOutput").ap()
    program(nc, aps)
    return run_bass_kernel_spmd(nc, [arrays], core_ids=[0]).results[0]["out"]
```
